# Optimizing a Trainium2 kernel written in Bass

```python
import numpy as np
import jax
import jax.numpy as jnp

def _softmax(x, axis=-1):
    return jax.nn.softmax(x, axis=axis)

def _gelu(x):
    return jax.nn.gelu(x, approximate=True)

def _silu(x):
    return jax.nn.silu(x)

def _sigmoid(x):
    return jax.nn.sigmoid(x)

def _layernorm(x, axis=-1, eps=1e-05):
    m = jnp.mean(x, axis=axis, keepdims=True)
    v = jnp.var(x, axis=axis, keepdims=True)
    return (x - m) / jnp.sqrt(v + eps)

def _scatter_add(tgt, idx, src, axis=0):
    return tgt.at[idx].add(src)

def _segment_sum(src, seg, n):
    return jax.ops.segment_sum(src, seg, n)
kernel_name = 'mk_prb_d1_jaxref_r8_1b20d5'

def setup_inputs(seed: int=0):
    np.random.seed(seed)
    _w = jnp.asarray

    def _L0_attn_setup():
        import jax, jax.numpy as jnp
        import numpy as np
        HIDDEN = 512
        N_HEADS = 32
        N_KV_HEADS = 8
        HEAD_DIM = HIDDEN // N_HEADS
        N_REP = N_HEADS // N_KV_HEADS
        KV_DIM = N_KV_HEADS * HEAD_DIM

        def _kaiming_uniform(key, out_f, in_f):
            bound = 1.0 / np.sqrt(in_f)
            return jax.random.uniform(key, (out_f, in_f), jnp.float32, -bound, bound)

        def bitnet_linear(x, weight, scale_param):
            s = jnp.maximum(jnp.mean(jnp.abs(weight), axis=1), 1e-08)
            binary_w = jnp.sign(weight / s[:, None])
            y = jnp.einsum('bsi,oi->bso', x, binary_w)
            y = y * (s * scale_param)[None, None, :]
            return jnp.nan_to_num(y, nan=0.0, posinf=1000000.0, neginf=-1000000.0)
        key = jax.random.key(seed)
        ks = jax.random.split(key, 5)
        return {'hidden_states': jax.random.normal(ks[0], (1, 256, HIDDEN), jnp.float32), 'q_weight': _kaiming_uniform(ks[1], HIDDEN, HIDDEN), 'q_scale': jnp.ones((HIDDEN,), jnp.float32), 'k_weight': _kaiming_uniform(ks[2], KV_DIM, HIDDEN), 'k_scale': jnp.ones((KV_DIM,), jnp.float32), 'v_weight': _kaiming_uniform(ks[3], KV_DIM, HIDDEN), 'v_scale': jnp.ones((KV_DIM,), jnp.float32), 'o_weight': _kaiming_uniform(ks[4], HIDDEN, HIDDEN), 'o_scale': jnp.ones((HIDDEN,), jnp.float32)}
    _L0_attn_in = _L0_attn_setup()

    def _L0_ffn_setup():
        import jax, jax.numpy as jnp
        import numpy as np
        H, FF = (512, 1792)
        B, S = (4, 256)
        key = jax.random.key(seed)
        ks = jax.random.split(key, 7)
        x = jax.random.normal(ks[0], (B, S, H), dtype=jnp.float32)
        gate_t = jax.random.randint(ks[1], (FF, H), -1, 2, dtype=jnp.int32)
        up_t = jax.random.randint(ks[2], (FF, H), -1, 2, dtype=jnp.int32)
        down_t = jax.random.randint(ks[3], (H, FF), -1, 2, dtype=jnp.int32)
        gate_s = jax.random.uniform(ks[4], (FF,), jnp.float32, 0.01, 0.1)
        up_s = jax.random.uniform(ks[5], (FF,), jnp.float32, 0.01, 0.1)
        down_s = jax.random.uniform(ks[6], (H,), jnp.float32, 0.01, 0.1)
        return {'x': x, 'gate_t': gate_t, 'up_t': up_t, 'down_t': down_t, 'gate_s': gate_s, 'up_s': up_s, 'down_s': down_s}
    _L0_ffn_in = _L0_ffn_setup()
    _d = {'L0_attn_hidden_states': _L0_attn_in['hidden_states'], 'L0_attn_q_weight': _L0_attn_in['q_weight'], 'L0_attn_q_scale': _L0_attn_in['q_scale'], 'L0_attn_k_weight': _L0_attn_in['k_weight'], 'L0_attn_k_scale': _L0_attn_in['k_scale'], 'L0_attn_v_weight': _L0_attn_in['v_weight'], 'L0_attn_v_scale': _L0_attn_in['v_scale'], 'L0_attn_o_weight': _L0_attn_in['o_weight'], 'L0_attn_o_scale': _L0_attn_in['o_scale'], 'L0_ffn_gate_t': _L0_ffn_in['gate_t'], 'L0_ffn_up_t': _L0_ffn_in['up_t'], 'L0_ffn_down_t': _L0_ffn_in['down_t'], 'L0_ffn_gate_s': _L0_ffn_in['gate_s'], 'L0_ffn_up_s': _L0_ffn_in['up_s'], 'L0_ffn_down_s': _L0_ffn_in['down_s']}
    _x0 = _d['L0_attn_hidden_states']
    _d['L0_attn_hidden_states'] = jax.random.normal(jax.random.fold_in(jax.random.key(seed), 1), (1, 1024, 512), dtype=_x0.dtype)
    del _x0
    return _d

def reference(L0_attn_hidden_states, L0_attn_q_weight, L0_attn_q_scale, L0_attn_k_weight, L0_attn_k_scale, L0_attn_v_weight, L0_attn_v_scale, L0_attn_o_weight, L0_attn_o_scale, L0_ffn_gate_t, L0_ffn_up_t, L0_ffn_down_t, L0_ffn_gate_s, L0_ffn_up_s, L0_ffn_down_s):

    def _L0_attn_ref(hidden_states, q_weight, q_scale, k_weight, k_scale, v_weight, v_scale, o_weight, o_scale):
        import jax, jax.numpy as jnp
        import numpy as np
        HIDDEN = 512
        N_HEADS = 32
        N_KV_HEADS = 8
        HEAD_DIM = HIDDEN // N_HEADS
        N_REP = N_HEADS // N_KV_HEADS
        KV_DIM = N_KV_HEADS * HEAD_DIM

        def _kaiming_uniform(key, out_f, in_f):
            bound = 1.0 / np.sqrt(in_f)
            return jax.random.uniform(key, (out_f, in_f), jnp.float32, -bound, bound)

        def bitnet_linear(x, weight, scale_param):
            s = jnp.maximum(jnp.mean(jnp.abs(weight), axis=1), 1e-08)
            binary_w = jnp.sign(weight / s[:, None])
            y = jnp.einsum('bsi,oi->bso', x, binary_w)
            y = y * (s * scale_param)[None, None, :]
            return jnp.nan_to_num(y, nan=0.0, posinf=1000000.0, neginf=-1000000.0)
        b, s, _ = hidden_states.shape
        q = bitnet_linear(hidden_states, q_weight, q_scale)
        k = bitnet_linear(hidden_states, k_weight, k_scale)
        v = bitnet_linear(hidden_states, v_weight, v_scale)
        q = q.reshape(b, s, N_HEADS, HEAD_DIM).transpose(0, 2, 1, 3)
        k = k.reshape(b, s, N_KV_HEADS, HEAD_DIM).transpose(0, 2, 1, 3)
        v = v.reshape(b, s, N_KV_HEADS, HEAD_DIM).transpose(0, 2, 1, 3)
        k = jnp.repeat(k, N_REP, axis=1)
        v = jnp.repeat(v, N_REP, axis=1)
        scores = jnp.einsum('bhqd,bhkd->bhqk', q, k) / np.sqrt(HEAD_DIM)
        attn = jax.nn.softmax(scores, axis=-1)
        out = jnp.einsum('bhqk,bhkd->bhqd', attn, v)
        out = out.transpose(0, 2, 1, 3).reshape(b, s, HIDDEN)
        return bitnet_linear(out, o_weight, o_scale)

    def _L0_ffn_ref(x, gate_t, up_t, down_t, gate_s, up_s, down_s):
        import jax, jax.numpy as jnp
        import numpy as np
        H, FF = (512, 1792)
        B, S = (4, 256)
        Bb, Ss, Hh = x.shape
        x_flat = x.reshape(Bb * Ss, Hh)
        gate_w = gate_t.astype(jnp.float32) * gate_s[:, None]
        up_w = up_t.astype(jnp.float32) * up_s[:, None]
        down_w = down_t.astype(jnp.float32) * down_s[:, None]
        gate_out = x_flat @ gate_w.T
        up_out = x_flat @ up_w.T
        hidden = jax.nn.silu(gate_out) * up_out
        out_flat = hidden @ down_w.T
        return out_flat.reshape(Bb, Ss, -1)
    x = L0_attn_hidden_states
    xn = _layernorm(x, axis=-1)
    x = x + _L0_attn_ref(xn, L0_attn_q_weight, L0_attn_q_scale, L0_attn_k_weight, L0_attn_k_scale, L0_attn_v_weight, L0_attn_v_scale, L0_attn_o_weight, L0_attn_o_scale) + _L0_ffn_ref(xn, L0_ffn_gate_t, L0_ffn_up_t, L0_ffn_down_t, L0_ffn_gate_s, L0_ffn_up_s, L0_ffn_down_s)
    return x

_drawn_inputs = setup_inputs


def setup_inputs(seed=0):
    import zlib

    import numpy as np

    out = dict(_drawn_inputs(seed))
    spreads = {'L0_attn_q_scale': (1.0, 0.6),
     'L0_attn_k_scale': (1.0, 0.6),
     'L0_attn_v_scale': (1.0, 0.6),
     'L0_attn_o_scale': (1.0, 0.6)}
    factors = {'L0_attn_q_weight': 8.0,
     'L0_attn_k_weight': 8.0,
     'L0_attn_v_weight': 8.0,
     'L0_attn_o_weight': 8.0}
    for name, (base, spread) in spreads.items():
        noise = np.random.default_rng([zlib.crc32(name.encode()), seed]).standard_normal(out[name].shape)
        drawn = base * np.exp(spread * noise) if base else spread * noise
        out[name] = jnp.asarray(drawn.astype(out[name].dtype))
    for name, factor in factors.items():
        out[name] = (out[name] * factor).astype(out[name].dtype)
    return out
```

```python
from contextlib import ExitStack

import concourse.bass as bass
from concourse import mybir

F32 = mybir.dt.float32
F16 = mybir.dt.float16
BF16 = mybir.dt.bfloat16
U8 = mybir.dt.uint8
ALU = mybir.AluOpType
ACT = mybir.ActivationFunctionType
AX = mybir.AxisListType
RMAX = bass.bass_isa.ReduceOp.max

P = 128
D = 16
EPS = 1e-5
SMALL = 1e-8
HUGE = 1e6


def layer_kernel(nc, x, wq, wk, wv, wo, sq, sk, sv, so, gate, up, down, sg, su, sd, out,
                 q_scratch, k_scratch, o_scratch, r_scratch):
    T, H = x.shape
    HC = H // P
    TT = T // P
    HALF = T // 2
    NH, NKV = wq.shape[1] // D, wk.shape[1] // D
    KV = NKV * D
    REP = NH // NKV
    FT = gate.shape[0]
    QT = NH * D // P
    HPT = P // D
    TERMS = 6
    KROWS = TERMS * D
    SROWS = KROWS + 3
    UNITS = REP * HALF // P
    NQKV = (NH + 2 * NKV) * D
    SCALE = float(D) ** -0.5
    NG = NKV
    NP = NG // 2
    STEPS = 2 * TT
    FU = 2 * FT

    assert KV == P and HC * P == H and QT * P == NH * D and TT % 4 == 0

    K_, V_ = "k", "v"
    PROJ = [K_, 0, V_] + list(range(1, QT))
    order = [("P", 0), ("P", 1), ("G", 0), ("F", 0), ("P", 2), ("F", 1), ("G", 1), ("F", 2), ("F", 3),
             ("P", 3), ("F", 4), ("G", 2), ("F", 5), ("F", 6), ("P", 4), ("G", 3), ("F", 7), ("F", 8),
             ("P", 5), ("G", 4), ("F", 9), ("F", 10), ("F", 11), ("G", 5)]
    done = 12
    for w in range(done, FU):
        order += [("F", w)]
        n = 2 * (w - done)
        order += [("A", n), ("A", n + 1)]
        if w == FU - 2:
            order += [("T", 0)]
    assert n + 2 == 2 * UNITS and len(PROJ) == 6

    def at(gp, s):
        gp = gp + s // (2 * STEPS)
        s = s % (2 * STEPS)
        return gp, s // STEPS, s % STEPS // TT, s % TT

    with ExitStack() as ctx:
        def sb(name, shape, dt):
            return ctx.enter_context(nc.sbuf_tensor(name, shape, dt))

        def sem(name):
            return ctx.enter_context(nc.semaphore(name))

        ps = ctx.enter_context(nc.psum_tensor("ps", [P, 8, 512], F32))

        def bank_pair(r):
            return ps[:, 2 * r:2 * r + 2, :].rearrange("p b n -> p (b n)")

        ident = sb("ident", [P, P], F32)
        ones = sb("ones", [P, P], F32)
        eps = sb("eps", [P, 1], F32)
        stats = sb("stats", [P, 2, 6], F32)
        mv = sb("mv", [P, TT, 2], F32)
        std = sb("std", [P, TT], F32)
        rstd = sb("rstd", [P, TT], F32)
        room1 = sb("room1", [P, HC * (NQKV + H)], F32)
        wt = room1[:, 0:HC * NQKV].rearrange("p (c n) -> p c n", c=HC)
        wot = room1[:, HC * NQKV:].rearrange("p (c n) -> p c n", c=HC)
        room2 = sb("room2", [P, 2 * REP * HALF], F32)
        xp = room2[:, :].bitcast(F16).rearrange("p (a c n) -> p a c n", a=2, c=HC)
        xhi, xlo = xp[:, 0], xp[:, 1]
        probs = room2[:, :].rearrange("p (b r n) -> p b r n", b=2, r=REP)
        att = room2[:, 0:2 * H].rearrange("p (b n) -> p b n", b=2)
        ffn = room2[:, 2 * H:4 * H].rearrange("p (b n) -> p b n", b=2)
        res = room2[:, 4 * H:6 * H].rearrange("p (b n) -> p b n", b=2)
        room3 = sb("room3", [P, 6 * HALF], F32)
        xin = room3[:, 0:4 * H].rearrange("p (b n) -> p b n", b=4)
        xn = room3[:, 4 * H:6 * H].rearrange("p (b n) -> p b n", b=2)
        th = room3[:, 0:2 * HALF].rearrange("p (b n) -> p b n", b=2)
        gt = room3[:, 2 * HALF:4 * HALF].rearrange("p (b n) -> p b n", b=2)
        hb = room3[:, 4 * HALF:6 * HALF].rearrange("p (b n) -> p b n", b=2)
        oparts = [room1[:, 0:9 * HALF].bitcast(BF16).rearrange("p (t a n) -> p t a n", t=3, a=3)[:, t] for t in range(3)]
        oparts += [room3[:, 0:3 * HALF].bitcast(BF16).rearrange("p (a n) -> p a n", a=3)]

        sgn = sb("sgn", [P, HC, NQKV], F16)
        sgno = sb("sgno", [P, HC, H], BF16)
        scqk = sb("scqk", [P, QT + 1], F32)
        cqk = sb("cqk", [P, QT + 1], F32)
        svb = sb("svb", [P, KV], F32)
        sob = sb("sob", [P, H], F32)
        dsb = sb("dsb", [P, H], F32)
        gsc = sb("gsc", [P, FT], F32)
        usc = sb("usc", [P, FT], F32)
        gain = sb("gain", [P, 4], F32)
        wf = sb("wf", [P, 2, 2, HC * P], F16)
        wd = sb("wd", [P, FT, H], F16)
        hhi = sb("hhi", [P, FT, T], F16)
        hlo = sb("hlo", [P, FT, T], F16)
        y = sb("y", [P, 2, T], F32)
        ga = sb("ga", [P, T], F32)
        gr = sb("gr", [P, T], F32)
        gb = sb("gb", [P, T], U8)
        parts = sb("parts", [P, 3, T], BF16)
        qst = sb("qst", [P, 2, 2, REP, HALF], BF16)
        kA = sb("kA", [P, 2, T], BF16)
        kB = sb("kB", [P, 2, T], BF16)
        vext = sb("vext", [P, TT, NKV, 2 * D], F32)
        vcur = sb("vcur", [P, 2, TT, 2 * D], F32)
        osb = sb("osb", [P, 2, HALF], F32)
        nmx = sb("nmx", [P, 2, UNITS], F32)
        shr = sb("shr", [UNITS, P], F32)
        shp = sb("shp", [UNITS, 2, 3, P], BF16)
        rsum = sb("rsum", [P, QT, T // D], F32)

        x_loaded = [sem(f"x_loaded{i}") for i in range(4)]
        qkv_loaded = sem("qkv_loaded")
        wo_loaded = sem("wo_loaded")
        vec_loaded = sem("vec_loaded")
        consts_ready = sem("consts_ready")
        kones_ready = sem("kones_ready")
        eps_ready = sem("eps_ready")
        pool_step = sem("pool_step")
        ln_step = sem("ln_step")
        stats_ready = sem("stats_ready")
        std_ready = sem("std_ready")
        xn_ready = sem("xn_ready")
        xT_ready = sem("xT_ready")
        xhi_ready = sem("xhi_ready")
        xlo_ready = sem("xlo_ready")
        sign_ready = sem("sign_ready")
        mag_ready = sem("mag_ready")
        sums_ready = sem("sums_ready")
        factor_step = sem("factor_step")
        factors_ready = sem("factors_ready")
        gain_ready = sem("gain_ready")
        gmax_ready = sem("gmax_ready")
        proj_ready = sem("proj_ready")
        y_ready = sem("y_ready")
        guard_step = sem("guard_step")
        guarded = sem("guarded")
        hi_ready = sem("hi_ready")
        rest_ready = sem("rest_ready")
        mid_ready = sem("mid_ready")
        split_done = sem("split_done")
        k_stored = sem("k_stored")
        q_stored = sem("q_stored")
        vext_ready = sem("vext_ready")
        vcur_ready = sem("vcur_ready")
        wf_loaded = [sem(f"wf_loaded{i}") for i in range(2)]
        wd_loaded = sem("wd_loaded")
        gate_ready = sem("gate_ready")
        up_ready = sem("up_ready")
        th_ready = sem("th_ready")
        gt_ready = sem("gt_ready")
        h_ready = sem("h_ready")
        hhi_ready = sem("hhi_ready")
        hlo_ready = sem("hlo_ready")
        q_loaded = [[sem(f"q_loaded{a}{b}") for b in range(2)] for a in range(2)]
        kA_loaded = [sem(f"kA_loaded{a}") for a in range(2)]
        kB_loaded = [sem(f"kB_loaded{a}") for a in range(2)]
        shift_loaded = [[sem(f"shift_loaded{a}{b}") for b in range(2)] for a in range(2)]
        rows_ready = sem("rows_ready")
        rows_free = sem("rows_free")
        maxT_ready = sem("maxT_ready")
        maxT_free = sem("maxT_free")
        shift_step = sem("shift_step")
        shift_ready = sem("shift_ready")
        scores_ready = sem("scores_ready")
        scores_free = sem("scores_free")
        probs_free = sem("probs_free")
        pv_free = sem("pv_free")
        osb_free = [sem(f"osb_free{i}") for i in range(2)]
        sums_loaded = sem("sums_loaded")
        rsum_ready = sem("rsum_ready")
        rsum_stored = sem("rsum_stored")
        num_loaded = [sem(f"num_loaded{i}") for i in range(2)]
        rec_loaded = sem("rec_loaded")
        normed = sem("normed")
        o_hi = sem("o_hi")
        o_rest = sem("o_rest")
        o_mid = sem("o_mid")
        o_split = sem("o_split")
        down_ready = sem("down_ready")
        oproj_ready = sem("oproj_ready")
        att_ready = sem("att_ready")
        ff_ready = sem("ff_ready")
        res_loaded = [sem(f"res_loaded{i}") for i in range(2)]
        res_added = sem("res_added")
        out_ready = sem("out_ready")
        out_stored = [sem(f"out_stored{i}") for i in range(2)]

        block = ctx.enter_context(nc.Block())

        @block.sync
        def _(sp):
            def load_queries(g, par, hf):
                src = q_scratch[bass.ds(g * REP, REP), :, :, hf * HALF:(hf + 1) * HALF]
                row = 0
                for n in (3, 2, 1):
                    sp.dma_start(qst[row:row + n * D, par, hf],
                                 src[:, 0:n].rearrange("h t d n -> (t d) h n")).then_inc(q_loaded[par][hf], 16)
                    row += n * D

            def load_keys(buf, loaded, g, par):
                sp.dma_start(buf[0:KROWS, par, :],
                             k_scratch[bass.ds(g, 1)].rearrange("g t d n -> (g t d) n")).then_inc(loaded[par], 16)

            def load_shift(v, par, hf):
                sp.wait_ge(shift_ready, v + 1)
                for part in range(3):
                    dst = qst[KROWS + part:KROWS + part + 1, par, hf].rearrange("p h n -> p (h n)")
                    sp.dma_start(dst, shp[:, hf, part, :]).then_inc(shift_loaded[par][hf], 16)

            sp.sem_inc(rows_free, 2)
            sp.sem_inc(maxT_free, 1)
            sp.sem_inc(scores_free, 2)
            sp.sem_inc(probs_free, 2)
            sp.sem_inc(pv_free, 1)
            for b in range(2):
                sp.sem_inc(osb_free[b], 16)

            x_v = x.rearrange("(i p) h -> i p h", p=P)
            for i in range(TT):
                if i >= 4:
                    sp.wait_ge(xn_ready, i - 3)
                sp.dma_start(xin[:, i % 4, :], x_v[i]).then_inc(x_loaded[i % 4], 16)

            splits = 0
            for what in PROJ:
                if what == V_:
                    continue
                splits += 1
                sp.wait_ge(mid_ready, splits)
                sp.wait_ge(split_done, splits)
                if what == K_:
                    for term, part in enumerate([0, 0, 0, 1, 1, 2]):
                        sp.dma_start(k_scratch[:, term], parts[:, part, :]).then_inc(k_stored, 16)
                    sp.wait_ge(k_stored, 16 * TERMS)
                    for par in range(2):
                        load_keys(kA, kA_loaded, par, par)
                        load_keys(kB, kB_loaded, par, par)
                else:
                    for part in range(3):
                        sp.dma_start(q_scratch[what * HPT:(what + 1) * HPT, part], parts[:, part, :]).then_inc(q_stored, 16)
                    if what == 0:
                        sp.wait_ge(q_stored, 48)
                        for g in range(2):
                            for hf in range(2):
                                load_queries(g, g, hf)
            sp.wait_ge(q_stored, 48 * QT)
            load_shift(0, 0, 0)

            def half_ended(gp, s, last):
                _, par, hf, _ = at(gp, s - 1)
                v = gp * 4 + s // TT - 1
                g = gp * 2 + par
                if not last:
                    sp.wait_ge(scores_ready, (v + 1) * REP * TT)
                    load_queries(g + 2, par, hf)
                    if hf == 0:
                        sp.wait_ge(rows_ready, (g + 1) * 2 * UNITS)
                        load_keys(kA, kA_loaded, g + 2, par)
                    else:
                        load_keys(kB, kB_loaded, g + 2, par)
                if not last or par == 0:
                    load_shift(v + 2, 1 - par, hf)
                sp.wait_ge(pv_free, v + 2)
                sp.dma_start(o_scratch[bass.ds(g * (REP * 2 * D), REP * 2 * D), hf * HALF:(hf + 1) * HALF],
                             osb[:, hf, :]).then_inc(osb_free[hf], 16)

            load_shift(1, 0, 1)
            for gp in range(NP - 1):
                for s in range(TT, 2 * STEPS + 1, TT):
                    half_ended(gp, s, False)

            def normalize_io(t):
                for hf in range(2):
                    sp.wait_ge(osb_free[hf], 16 * (2 * t + 3))
                heads = o_scratch.rearrange("(h z d) n -> h z d n", z=2, d=D)[t * HPT:(t + 1) * HPT]
                sp.dma_start(rsum[:, t, :], heads[:, 1, 0].rearrange("h (b n) -> h b n", b=D)).then_inc(sums_loaded, 16)
                if t >= 2:
                    sp.wait_ge(o_split, t - 1)
                sp.dma_start(y[:, t % 2, :], heads[:, 0]).then_inc(num_loaded[t % 2], 16)
                sp.wait_ge(rsum_ready, t + 1)
                sp.dma_start(r_scratch[t * HPT:(t + 1) * HPT].rearrange("h (b n) -> h b n", b=D),
                             rsum[:, t, :]).then_inc(rsum_stored, 16)
                sp.wait_ge(rsum_stored, 16 * (t + 1))
                if t >= 1:
                    sp.wait_ge(normed, t)
                rec = r_scratch[t * HPT:(t + 1) * HPT].unsqueeze(1).to_broadcast([HPT, D, T])
                sp.dma_start(ga[:, :], rec).then_inc(rec_loaded, 16)

            for s in range(TT, 2 * STEPS + 1, TT):
                half_ended(NP - 1, s, True)
                if s == STEPS + TT // 1:
                    for t in range(QT - 1):
                        normalize_io(t)
            normalize_io(QT - 1)
            def store(i):
                sp.wait_ge(out_ready, i + 1)
                sp.dma_start(out.rearrange("(i p) h -> i p h", p=P)[i], ffn[:, i % 2, :]).then_inc(out_stored[i % 2], 16)

            for i in range(TT):
                if i >= 2:
                    sp.wait_ge(res_added, i - 1)
                sp.dma_start(res[:, i % 2, :], x_v[i]).then_inc(res_loaded[i % 2], 16)
                if i >= 1:
                    store(i - 1)
            store(TT - 1)
            for b in range(2):
                sp.wait_ge(out_stored[b], 16 * TT // 2)

        @block.gpsimd
        def _(pool):
            def load_ffn(f):
                pool.dma_start(wf[:, f % 2, 0, :], gate[f]).then_inc(wf_loaded[f % 2], 16)
                pool.dma_start(wf[:, f % 2, 1, :], up[f]).then_inc(wf_loaded[f % 2], 16)

            nc.gpsimd.memset(ident[:, :], 0.0).then_inc(pool_step, 1)
            pool.wait_ge(pool_step, 1)
            nc.gpsimd.affine_select(out=ident[:, :], in_=ident[:, :], compare_op=ALU.not_equal, fill=1.0, base=0,
                                    pattern=[[-1, P]], channel_multiplier=1).then_inc(consts_ready, 1)
            nc.gpsimd.memset(ones[:, :], 1.0).then_inc(consts_ready, 1)
            load_ffn(0)
            load_ffn(1)
            nc.gpsimd.memset(vext[:, :, :, :], 1.0).then_inc(consts_ready, 1)
            pool.wait_ge(gain_ready, 1)
            nc.gpsimd.partition_all_reduce(gain[:, 1:2], gain[:, 0:1], P, RMAX).then_inc(gmax_ready, 1)

            for kind, w in order:
                if kind != "F":
                    continue
                f, hf = w // 2, w % 2
                if hf == 0 and 1 <= f < FT - 1:
                    pool.wait_ge(up_ready, w)
                    load_ffn(f + 1)
                if w == 3:
                    pool.dma_start(wd[:, :, :], down.rearrange("(f p) h -> p f h", p=P)).then_inc(wd_loaded, 16)
                pool.wait_ge(hhi_ready, w + 1)
                nc.gpsimd.tensor_tensor(hlo[:, f, hf * HALF:(hf + 1) * HALF], hb[:, w % 2, :],
                                        hhi[:, f, hf * HALF:(hf + 1) * HALF], ALU.subtract).then_inc(hlo_ready, 1)
            pool.wait_ge(vext_ready, 1)
            for g in range(2):
                nc.gpsimd.tensor_copy(vcur[:, g, :, :], vext[:, :, g, :]).then_inc(vcur_ready, 1)
            for g in range(2, NG):
                pool.wait_ge(probs_free, 2 + STEPS * (g - 1))
                nc.gpsimd.tensor_copy(vcur[:, g % 2, :, :], vext[:, :, g, :]).then_inc(vcur_ready, 1)
            for t in range(QT):
                pool.wait_ge(normed, t + 1)
                nc.gpsimd.tensor_copy(oparts[t][:, 0, :], y[:, t % 2, :]).then_inc(o_hi, 1)
                pool.wait_ge(o_rest, t + 1)
                nc.gpsimd.tensor_copy(oparts[t][:, 1, :], y[:, t % 2, :]).then_inc(o_mid, 1)
            for i in range(TT):
                pool.wait_ge(ff_ready, i + 1)
                pool.wait_ge(res_loaded[i % 2], 16 * (i // 2 + 1))
                nc.gpsimd.tensor_tensor(ffn[:, i % 2, :], ffn[:, i % 2, :], res[:, i % 2, :], ALU.add).then_inc(res_added, 1)

        @block.scalar
        def _(act):
            for w_, c0 in ((wk, NH * D), (wq, 0), (wv, NH * D + KV)):
                act.dma_start(wt[:, :, c0:c0 + w_.shape[1]],
                              w_.rearrange("(c p) o -> p c o", p=P)).then_inc(qkv_loaded, 16)
            act.dma_start(scqk[:, 0:QT], sq).then_inc(vec_loaded, 16)
            act.dma_start(scqk[:, QT:QT + 1], sk).then_inc(vec_loaded, 16)
            act.dma_start(svb[:, :], sv.to_broadcast([P, KV])).then_inc(vec_loaded, 16)
            act.dma_start(sob[:, :], so.to_broadcast([P, H])).then_inc(vec_loaded, 16)
            act.dma_start(dsb[:, :], sd.to_broadcast([P, H])).then_inc(vec_loaded, 16)
            act.dma_start(gsc[:, :], sg).then_inc(vec_loaded, 16)
            act.dma_start(usc[:, :], su).then_inc(vec_loaded, 16)
            act.dma_start(wot[:, :, :], wo.rearrange("(c p) o -> p c o", p=P)).then_inc(wo_loaded, 16)

            def xhi_copy(i):
                act.wait_ge(xT_ready, i + 1)
                nc.scalar.copy(xhi[:, :, i * P:(i + 1) * P],
                               ps[:, i % 2, :].rearrange("p (c n) -> p c n", c=HC)).then_inc(xhi_ready, 1)

            act.wait_ge(eps_ready, 1)
            for i in range(TT):
                act.wait_ge(stats_ready, i + 1)
                nc.scalar.activation(std[:, i:i + 1], mv[:, i, 1:2], ACT.Sqrt, bias=eps[:, 0:1]).then_inc(std_ready, 1)
                if i >= 1:
                    xhi_copy(i - 1)
                if i == 2:
                    act.wait_ge(qkv_loaded, 48)
                    nc.scalar.activation(sgn[:, :, :], wt, ACT.Sign).then_inc(sign_ready, 1)
                if i == 4:
                    act.wait_ge(sign_ready, 1)
                    nc.scalar.activation(wt, wt, ACT.Abs).then_inc(mag_ready, 1)
            xhi_copy(TT - 1)
            act.wait_ge(wo_loaded, 16)
            nc.scalar.activation(sgno[:, :, :], wot, ACT.Sign).then_inc(sign_ready, 1)
            act.wait_ge(sign_ready, 2)
            nc.scalar.activation(wot, wot, ACT.Abs).then_inc(mag_ready, 1)

            splits = 0
            for kind, n in order:
                if kind == "P" and PROJ[n] != V_:
                    col = QT if PROJ[n] == K_ else PROJ[n]
                    act.wait_ge(proj_ready, n + 1)
                    act.wait_ge(factors_ready, 1)
                    if n >= 2:
                        act.wait_ge(split_done, sum(1 for m in PROJ[:n - 1] if m != V_))
                        act.wait_ge(guarded, n - 1)
                    nc.scalar.activation(y[:, n % 2, :], bank_pair(n % 2), ACT.Copy,
                                         scale=cqk[:, col:col + 1]).then_inc(y_ready, 1)
                elif kind == "G" and PROJ[n] == V_:
                    act.wait_ge(guarded, n + 1)
                    act.wait_ge(consts_ready, 3)
                    nc.scalar.copy(vext[:, :, :, 0:D].rearrange("p k g d -> p (k g) d"),
                                   y[:, n % 2, :].rearrange("p (m d) -> p m d", d=D)).then_inc(vext_ready, 1)
                elif kind == "G":
                    splits += 1
                    act.wait_ge(guarded, n + 1)
                    if splits == 2:
                        act.wait_ge(k_stored, 16 * TERMS)
                    elif splits > 2:
                        act.wait_ge(q_stored, 48 * (splits - 2))
                    nc.scalar.copy(parts[:, 0, :], y[:, n % 2, :]).then_inc(hi_ready, 1)
                    act.wait_ge(rest_ready, splits)
                    nc.scalar.copy(parts[:, 1, :], gr[:, :]).then_inc(mid_ready, 1)
                elif kind == "F":
                    f, hf = n // 2, n % 2
                    act.wait_ge(gate_ready, n + 1)
                    if n >= 2:
                        act.wait_ge(gt_ready, n - 1)
                    nc.scalar.activation(th[:, n % 2, :], ps[:, 4 + 2 * (n % 2), :], ACT.Tanh,
                                         scale=gsc[:, f:f + 1]).then_inc(th_ready, 1)
                    act.wait_ge(h_ready, n + 1)
                    nc.scalar.copy(hhi[:, f, hf * HALF:(hf + 1) * HALF], hb[:, n % 2, :]).then_inc(hhi_ready, 1)

            def exps(gp, s):
                _, _, _, kt = at(gp, s)
                step = gp * (2 * STEPS) + s
                act.wait_ge(probs_free, step + 1)
                for r in range(REP):
                    act.wait_ge(scores_ready, step * REP + r + 1)
                    nc.scalar.activation(probs[:, s % 2, r, :], ps[:, 4 + r % 2, :], ACT.Exp,
                                         scale=SCALE).then_inc(scores_free, 1)

            def take_output(gp, s):
                _, par, hf, _ = at(gp, s - 1)
                v = gp * 4 + s // TT - 1
                act.wait_ge(probs_free, (v + 1) * TT + 2)
                act.wait_ge(osb_free[hf], 16 * (gp * 2 + par + 1))
                nc.scalar.copy(osb[:, hf, :], ps[:, 6, :]).then_inc(pv_free, 1)

            act.wait_ge(hlo_ready, FU)
            exps(0, 0)
            for gp in range(NP):
                for s in range(1, 2 * STEPS + 1):
                    if not (gp == NP - 1 and s == 2 * STEPS):
                        exps(gp, s)
                    if s % TT == 0:
                        take_output(gp, s)

        @block.vector
        def _(dve):
            nc.vector.memset(eps[:, :], EPS).then_inc(eps_ready, 1)
            nc.vector.memset(kB[KROWS:P, :, :], 1.0).then_inc(kones_ready, 1)

            ln = 0

            def x_stats(i):
                nonlocal ln
                dve.wait_ge(x_loaded[i % 4], 16 * (i // 4 + 1))
                nc.vector.bn_stats(stats[:, i % 2, :], xin[:, i % 4, :]).then_inc(ln_step, 1)
                ln += 1
                dve.wait_ge(ln_step, ln)
                nc.vector.bn_aggr(mv[:, i, :], stats[:, i % 2, :]).then_inc(stats_ready, 1)

            def normalize(i):
                nonlocal ln
                dve.wait_ge(std_ready, i + 1)
                nc.vector.reciprocal(rstd[:, i:i + 1], std[:, i:i + 1]).then_inc(ln_step, 1)
                ln += 1
                dve.wait_ge(ln_step, ln)
                if i >= 2:
                    dve.wait_ge(xT_ready, i - 1)
                nc.vector.tensor_scalar(xn[:, i % 2, :], xin[:, i % 4, :], mv[:, i, 0:1], rstd[:, i:i + 1],
                                        ALU.subtract, ALU.mult).then_inc(xn_ready, 1)

            def x_low(i):
                dve.wait_ge(xhi_ready, i + 1)
                nc.vector.tensor_tensor(xlo[:, :, i * P:(i + 1) * P],
                                        ps[:, i % 2, :].rearrange("p (c n) -> p c n", c=HC),
                                        xhi[:, :, i * P:(i + 1) * P], ALU.subtract).then_inc(xlo_ready, 1)

            x_stats(0)
            for i in range(TT):
                if i + 1 < TT:
                    x_stats(i + 1)
                normalize(i)
                if i >= 1:
                    x_low(i - 1)
            x_low(TT - 1)

            steps = 0

            def step(ins):
                nonlocal steps
                steps += 1
                ins.then_inc(factor_step, 1)
                dve.wait_ge(factor_step, steps)

            dve.wait_ge(vec_loaded, 16 * 7)
            dve.wait_ge(sums_ready, 1)
            step(nc.vector.tensor_scalar(cqk[:, :], ps[:, 7, 0:QT + 1], 1.0 / H, SMALL, ALU.mult, ALU.max))
            nc.vector.tensor_tensor(cqk[:, :], cqk[:, :], scqk[:, :], ALU.mult).then_inc(factors_ready, 1)
            step(nc.vector.tensor_scalar(ga[:, 0:KV], ps[:, 7, KV:2 * KV], 1.0 / H, SMALL, ALU.mult, ALU.max))
            nc.vector.tensor_tensor(svb[:, :], ga[:, 0:KV], svb[:, :], ALU.mult).then_inc(factors_ready, 1)
            step(nc.vector.tensor_tensor(usc[:, :], usc[:, :], gsc[:, :], ALU.mult))
            nc.vector.tensor_reduce(gain[:, 0:1], usc[:, :], AX.X, ALU.max, apply_absolute_value=True).then_inc(gain_ready, 1)
            step(nc.vector.tensor_scalar(gsc[:, :], gsc[:, :], 0.5, None, ALU.mult))
            dve.wait_ge(gmax_ready, 1)
            step(nc.vector.tensor_scalar(gain[:, 2:3], gain[:, 1:2], 8.0, 1e-30, ALU.mult, ALU.max))
            step(nc.vector.reciprocal(gain[:, 3:4], gain[:, 2:3]))
            step(nc.vector.tensor_scalar(usc[:, :], usc[:, :], gain[:, 3:4], 0.5, ALU.mult, ALU.mult))
            nc.vector.tensor_scalar(dsb[:, :], dsb[:, :], gain[:, 2:3], None, ALU.mult).then_inc(factors_ready, 1)
            dve.wait_ge(sums_ready, 2)
            step(nc.vector.tensor_scalar(ga[:, 0:H], ps[:, 6, :], 1.0 / H, SMALL, ALU.mult, ALU.max))
            nc.vector.tensor_tensor(sob[:, :], ga[:, 0:H], sob[:, :], ALU.mult).then_inc(factors_ready, 1)

            guards = 0

            def guard(v_, n_):
                nonlocal guards
                mask, repl, same = gb[:, 0:n_], ga[:, 0:n_], gr[:, 0:n_]
                nc.vector.tensor_scalar(mask, v_, 0.0, 0.0, ALU.mult, ALU.not_equal).then_inc(guard_step, 1)
                nc.vector.tensor_scalar(repl, v_, HUGE, -HUGE, ALU.min, ALU.max).then_inc(guard_step, 1)
                nc.vector.tensor_tensor(same, v_, v_, ALU.is_equal).then_inc(guard_step, 1)
                dve.wait_ge(guard_step, guards + 3)
                nc.vector.tensor_tensor(repl, repl, same, ALU.mult).then_inc(guard_step, 1)
                guards += 4
                dve.wait_ge(guard_step, guards)
                return nc.vector.copy_predicated(v_, mask, repl)

            def row_max(n, hf, idx):
                dve.wait_ge(rows_ready, n + 1)
                nc.vector.tensor_reduce(nmx[:, hf, idx:idx + 1], bank_pair(idx % 2), AX.X, ALU.max,
                                        negate=True).then_inc(rows_free, 1)

            def split_max(v, hf):
                dve.wait_ge(maxT_ready, v + 1)
                nc.vector.tensor_copy(shp[:, hf, 0, :], ps[0:UNITS, 7, 0:P]).then_inc(shift_step, 1)
                dve.wait_ge(shift_step, 2 * v + 1)
                nc.vector.tensor_tensor(shr[:, :], ps[0:UNITS, 7, 0:P], shp[:, hf, 0, :], ALU.subtract).then_inc(maxT_free, 1)
                dve.wait_ge(maxT_free, v + 2)
                nc.vector.tensor_copy(shp[:, hf, 1, :], shr[:, :]).then_inc(shift_step, 1)
                dve.wait_ge(shift_step, 2 * v + 2)
                nc.vector.tensor_tensor(shp[:, hf, 2, :], shr[:, :], shp[:, hf, 1, :], ALU.subtract).then_inc(shift_ready, 1)

            splits = 0
            for kind, n in order:
                if kind == "P" and PROJ[n] == V_:
                    dve.wait_ge(proj_ready, n + 1)
                    dve.wait_ge(factors_ready, 2)
                    dve.wait_ge(mid_ready, splits)
                    nc.vector.tensor_tensor(y[:, n % 2, :].rearrange("p (k m) -> p k m", m=KV),
                                            bank_pair(n % 2).rearrange("p (k m) -> p k m", m=KV),
                                            svb[:, :].unsqueeze(1).to_broadcast([P, TT, KV]),
                                            ALU.mult).then_inc(y_ready, 1)
                elif kind == "G":
                    dve.wait_ge(y_ready, n + 1)
                    if n == 0:
                        dve.wait_ge(factors_ready, 4)
                    else:
                        dve.wait_ge(guarded, n)
                        dve.wait_ge(split_done, splits)
                    guard(y[:, n % 2, :], T).then_inc(guarded, 1)
                    if PROJ[n] == V_:
                        continue
                    splits += 1
                    dve.wait_ge(hi_ready, splits)
                    nc.vector.tensor_tensor(gr[:, :], y[:, n % 2, :], parts[:, 0, :], ALU.subtract).then_inc(rest_ready, 1)
                    dve.wait_ge(mid_ready, splits)
                    nc.vector.tensor_tensor(parts[:, 2, :], gr[:, :], parts[:, 1, :], ALU.subtract).then_inc(split_done, 1)
                elif kind == "F":
                    f, hf = n // 2, n % 2
                    dve.wait_ge(th_ready, n + 1)
                    nc.vector.scalar_tensor_tensor(out=gt[:, n % 2, :], in0=th[:, n % 2, :], scalar=1.0,
                                                   in1=ps[:, 4 + 2 * (n % 2), :], op0=ALU.add,
                                                   op1=ALU.mult).then_inc(gt_ready, 1)
                    dve.wait_ge(gt_ready, n + 1)
                    dve.wait_ge(up_ready, n + 1)
                    if n >= 2:
                        dve.wait_ge(hlo_ready, n - 1)
                    nc.vector.scalar_tensor_tensor(out=hb[:, n % 2, :], in0=ps[:, 5 + 2 * (n % 2), :],
                                                   scalar=usc[:, f:f + 1], in1=gt[:, n % 2, :],
                                                   op0=ALU.mult, op1=ALU.mult).then_inc(h_ready, 1)
                elif kind == "A":
                    row_max(n, n // UNITS, n % UNITS)
                elif kind == "T":
                    split_max(0, 0)

            def step_rows(gp, s, last):
                gp_, par, hf, kt = at(gp, s)
                if not (last and (par == 1 or s == 2 * STEPS)):
                    ga_ = gp_ * 2 + par + 1
                    for j in range(2):
                        idx = 2 * kt + j
                        row_max(ga_ * (2 * UNITS) + hf * UNITS + idx, hf, idx)
                if s % TT == 0 and not (last and s >= STEPS + TT):
                    v = gp * 4 + s // TT + 1
                    if s > 0:
                        _, ppar, phf, _ = at(gp, s - 1)
                        dve.wait_ge(shift_loaded[ppar][phf], 48 * (gp + 1))
                    else:
                        phf = 1
                    split_max(v, phf)

            step_rows(0, 0, False)
            for gp in range(NP):
                for s in range(1, 2 * STEPS + 1):
                    if gp == NP - 1 and s == 2 * STEPS:
                        break
                    step_rows(gp, s, gp == NP - 1)
                    
            for t in range(QT):
                dve.wait_ge(sums_loaded, 16 * (t + 1))
                nc.vector.reciprocal(rsum[:, t, :], rsum[:, t, :]).then_inc(rsum_ready, 1)
                dve.wait_ge(num_loaded[t % 2], 16 * (t // 2 + 1))
                dve.wait_ge(rec_loaded, 16 * (t + 1))
                nc.vector.tensor_tensor(y[:, t % 2, :], y[:, t % 2, :], ga[:, :], ALU.mult).then_inc(normed, 1)
                dve.wait_ge(o_hi, t + 1)
                nc.vector.tensor_tensor(y[:, t % 2, :], y[:, t % 2, :], oparts[t][:, 0, :], ALU.subtract).then_inc(o_rest, 1)
                dve.wait_ge(o_mid, t + 1)
                nc.vector.tensor_tensor(oparts[t][:, 2, :], y[:, t % 2, :], oparts[t][:, 1, :], ALU.subtract).then_inc(o_split, 1)

            for i in range(TT):
                dve.wait_ge(down_ready, i + 1)
                if i >= 2:
                    dve.wait_ge(out_stored[i % 2], 16 * (i // 2))
                nc.vector.tensor_tensor(ffn[:, i % 2, :], ps[:, 2 * (i % 4), :], dsb[:, :], ALU.mult).then_inc(ff_ready, 1)
                dve.wait_ge(oproj_ready, i + 1)
                nc.vector.tensor_tensor(att[:, i % 2, :], ps[:, 2 * (i % 4) + 1, :], sob[:, :], ALU.mult).then_inc(att_ready, 1)
                dve.wait_ge(att_ready, 2 * i + 1)
                guard(att[:, i % 2, :], H).then_inc(att_ready, 1)
                dve.wait_ge(att_ready, 2 * i + 2)
                dve.wait_ge(res_added, i + 1)
                nc.vector.tensor_tensor(ffn[:, i % 2, :], ffn[:, i % 2, :], att[:, i % 2, :], ALU.add).then_inc(out_ready, 1)

        @block.tensor
        def _(pe):
            pe.wait_ge(consts_ready, 1)
            for i in range(TT):
                pe.wait_ge(xn_ready, i + 1)
                if i >= 2:
                    pe.wait_ge(xlo_ready, i - 1)
                for c in range(HC):
                    mm = nc.tensor.transpose(ps[:, i % 2, c * P:(c + 1) * P], xn[:, i % 2, c * P:(c + 1) * P], ident[:, :])
                mm.then_inc(xT_ready, 1)

            pe.wait_ge(mag_ready, 1)
            pe.wait_ge(consts_ready, 2)
            for col in range(QT + 1):
                for c in range(HC):
                    mm = nc.tensor.matmul(ps[:, 7, col:col + 1], wt[:, c, col * P:(col + 1) * P], ones[:, 0:1],
                                          start=(c == 0), stop=(c == HC - 1))
            for c in range(HC):
                mm = nc.tensor.matmul(ps[:, 7, KV:2 * KV], ones[:, :], wt[:, c, NH * D + KV:NQKV],
                                      start=(c == 0), stop=(c == HC - 1))
            mm.then_inc(sums_ready, 1)
            pe.wait_ge(mag_ready, 2)
            for c in range(HC):
                mm = nc.tensor.matmul(ps[:, 6, :], ones[:, :], wot[:, c, :], start=(c == 0), stop=(c == HC - 1))
            mm.then_inc(sums_ready, 1)

            def project(n):
                what = PROJ[n]
                pe.wait_ge(sign_ready, 1)
                pe.wait_ge(xlo_ready, TT)
                if n >= 2:
                    pe.wait_ge(y_ready, n - 1)
                if what == V_:
                    for k in range(TT):
                        for c in range(HC):
                            for xs in (xhi, xlo):
                                mm = nc.tensor.matmul(bank_pair(n % 2)[:, k * KV:(k + 1) * KV], xs[:, c, k * P:(k + 1) * P],
                                                      sgn[:, c, NH * D + KV:NQKV], start=(c == 0 and xs is xhi),
                                                      stop=(c == HC - 1 and xs is xlo))
                else:
                    c0 = NH * D if what == K_ else what * P
                    for hf in range(2):
                        for c in range(HC):
                            for xs in (xhi, xlo):
                                mm = nc.tensor.matmul(ps[:, 2 * (n % 2) + hf, :], sgn[:, c, c0:c0 + P],
                                                      xs[:, c, hf * HALF:(hf + 1) * HALF],
                                                      start=(c == 0 and xs is xhi), stop=(c == HC - 1 and xs is xlo))
                mm.then_inc(proj_ready, 1)

            def feed_forward(w):
                f, hf = w // 2, w % 2
                pe.wait_ge(wf_loaded[f % 2], 32 * (f // 2 + 1))
                if w < 2:
                    pe.wait_ge(factors_ready, 4)
                else:
                    pe.wait_ge(h_ready, w - 1)
                if w == FU - 1:
                    pe.wait_ge(maxT_free, 2)
                for z, ready in ((0, gate_ready), (1, up_ready)):
                    for c in range(HC):
                        for xs in (xhi, xlo):
                            mm = nc.tensor.matmul(ps[:, 4 + 2 * (w % 2) + z, :], wf[:, f % 2, z, c * P:(c + 1) * P],
                                                  xs[:, c, hf * HALF:(hf + 1) * HALF],
                                                  start=(c == 0 and xs is xhi), stop=(c == HC - 1 and xs is xlo))
                    mm.then_inc(ready, 1)

            def rows(n, par, hf, idx):
                head, qt = idx // (HALF // P), idx % (HALF // P)
                pe.wait_ge(rows_free, n + 1)
                for b in range(2):
                    mm = nc.tensor.matmul(ps[:, 2 * (idx % 2) + b, :], qst[0:KROWS, par, hf, head, qt * P:(qt + 1) * P],
                                          kA[0:KROWS, par, b * HALF:(b + 1) * HALF], start=True, stop=True)
                mm.then_inc(rows_ready, 1)

            def transpose_max(v, hf):
                pe.wait_ge(rows_free, 2 + (v + 1) * UNITS)
                pe.wait_ge(maxT_free, v + 1)
                nc.tensor.transpose(ps[0:UNITS, 7, 0:P], nmx[:, hf, :], ident[:, :]).then_inc(maxT_ready, 1)

            for kind, n in order:
                if kind == "P":
                    project(n)
                elif kind == "F":
                    feed_forward(n)
                elif kind == "A":
                    if n == 0:
                        pe.wait_ge(y_ready, len(PROJ))
                        pe.wait_ge(kA_loaded[0], 16)
                    if n % UNITS == 0:
                        pe.wait_ge(q_loaded[0][n // UNITS], 48)
                    rows(n, 0, n // UNITS, n % UNITS)
                elif kind == "T":
                    pe.wait_ge(h_ready, FU - 2)
                    transpose_max(0, 0)

            def scores(gp, s, last):
                gp_, par, hf, kt = at(gp, s)
                step_ = gp * (2 * STEPS) + s
                if kt == 0:
                    pe.wait_ge(q_loaded[par][hf], 48 * (gp_ + 1))
                    pe.wait_ge(shift_loaded[par][hf], 48 * (gp_ + 1))
                    if hf == 0:
                        pe.wait_ge(kB_loaded[par], 16 * (gp_ + 1))
                with_rows = not (last and par == 1)
                if with_rows and kt == 0:
                    pe.wait_ge(q_loaded[1 - par][hf], 48 * (gp_ + par + 1))
                    if hf == 0:
                        pe.wait_ge(kA_loaded[1 - par], 16 * (gp_ + par + 1))
                for r in range(REP):
                    pe.wait_ge(scores_free, step_ * REP + r + 1)
                    nc.tensor.matmul(ps[:, 4 + r % 2, :], kB[0:SROWS, par, kt * P:(kt + 1) * P],
                                     qst[0:SROWS, par, hf, r, :], start=True, stop=True).then_inc(scores_ready, 1)
                    if with_rows and r % 2 == 1:
                        idx = 2 * kt + r // 2
                        rows((gp_ * 2 + par + 1) * (2 * UNITS) + hf * UNITS + idx, 1 - par, hf, idx)
                if kt == 0 and not (last and s >= STEPS + TT):
                    transpose_max(gp * 4 + s // TT + 1, 1 - hf)

            def times_values(gp, s):
                gp_, par, hf, kt = at(gp, s)
                step_ = gp * (2 * STEPS) + s
                if kt == 0:
                    pe.wait_ge(pv_free, gp * 4 + s // TT + 1)
                    if hf == 0:
                        pe.wait_ge(vcur_ready, gp * 2 + par + 1)
                pe.wait_ge(scores_free, 2 + (step_ + 1) * REP)
                for r in range(REP):
                    mm = nc.tensor.matmul(ps[32 * r:32 * r + 32, 6, :], vcur[:, par, kt, :], probs[:, s % 2, r, :],
                                          start=(kt == 0), stop=(kt == TT - 1))
                mm.then_inc(probs_free, 1)

            pe.wait_ge(h_ready, FU)
            pe.wait_ge(kones_ready, 1)
            scores(0, 0, False)
            for gp in range(NP):
                last = gp == NP - 1
                for s in range(2 * STEPS):
                    if not (last and s == 2 * STEPS - 1):
                        scores(gp, s + 1, last)
                    times_values(gp, s)

            pe.wait_ge(wd_loaded, 16)
            pe.wait_ge(pv_free, 2 * NG + 1)
            def down_proj(i):
                if i >= 4:
                    pe.wait_ge(ff_ready, i - 3)
                for f in range(FT):
                    for hs in (hhi, hlo):
                        mm = nc.tensor.matmul(ps[:, 2 * (i % 4), :], hs[:, f, i * P:(i + 1) * P], wd[:, f, :],
                                              start=(f == 0 and hs is hhi), stop=(f == FT - 1 and hs is hlo))
                mm.then_inc(down_ready, 1)

            def out_proj(i):
                if i == 0:
                    pe.wait_ge(o_split, QT)
                    pe.wait_ge(o_mid, QT)
                if i >= 4:
                    pe.wait_ge(att_ready, 2 * (i - 4) + 1)
                for t in range(QT):
                    for part in range(3):
                        mm = nc.tensor.matmul(ps[:, 2 * (i % 4) + 1, :], oparts[t][:, part, i * P:(i + 1) * P], sgno[:, t, :],
                                              start=(t == 0 and part == 0), stop=(t == QT - 1 and part == 2))
                mm.then_inc(oproj_ready, 1)

            AHEAD = 2
            for i in range(TT + AHEAD):
                if i < TT:
                    down_proj(i)
                if i >= AHEAD:
                    out_proj(i - AHEAD)


_INS = ["x", "wq", "wk", "wv", "wo", "sq", "sk", "sv", "so", "gate", "up", "down", "sg", "su", "sd"]


def kernel(L0_attn_hidden_states, L0_attn_q_weight, L0_attn_q_scale, L0_attn_k_weight, L0_attn_k_scale,
           L0_attn_v_weight, L0_attn_v_scale, L0_attn_o_weight, L0_attn_o_scale, L0_ffn_gate_t, L0_ffn_up_t,
           L0_ffn_down_t, L0_ffn_gate_s, L0_ffn_up_s, L0_ffn_down_s):
    import numpy as np
    import concourse.bacc as bacc
    from concourse.bass_utils import run_bass_kernel_spmd

    _, T, H = L0_attn_hidden_states.shape
    FT = L0_ffn_gate_t.shape[0] // P

    def columns(v):
        return np.ascontiguousarray(np.asarray(v).reshape(-1, P).T)

    def tiles(w):
        w = np.asarray(w).reshape(FT, P, H // P, P)
        return np.ascontiguousarray(w.transpose(0, 3, 2, 1)).reshape(FT, P, H)

    def turned(w):
        return np.ascontiguousarray(np.asarray(w).T)

    def row(v):
        return np.ascontiguousarray(np.asarray(v).reshape(1, -1))

    arrays = {
        "x": np.ascontiguousarray(np.asarray(L0_attn_hidden_states).reshape(T, H)),
        "wq": turned(L0_attn_q_weight), "wk": turned(L0_attn_k_weight),
        "wv": turned(L0_attn_v_weight), "wo": turned(L0_attn_o_weight),
        "sq": columns(L0_attn_q_scale), "sk": columns(L0_attn_k_scale),
        "sv": row(L0_attn_v_scale), "so": row(L0_attn_o_scale),
        "gate": tiles(L0_ffn_gate_t), "up": tiles(L0_ffn_up_t), "down": turned(L0_ffn_down_t),
        "sg": columns(L0_ffn_gate_s), "su": columns(L0_ffn_up_s), "sd": row(L0_ffn_down_s),
    }
    NH = arrays["wq"].shape[1] // D
    NKV = arrays["wk"].shape[1] // D
    nc = bacc.Bacc("TRN2", target_bir_lowering=False, num_devices=1)
    args = [nc.dram_tensor(n, arrays[n].shape, mybir.dt.from_np(arrays[n].dtype), kind="ExternalInput").ap() for n in _INS]
    args.append(nc.dram_tensor("out", (T, H), F32, kind="ExternalOutput").ap())
    args.append(nc.dram_tensor("q_scratch", (NH, 3, D, T), BF16, kind="Internal").ap())
    args.append(nc.dram_tensor("k_scratch", (NKV, 6, D, T), BF16, kind="Internal").ap())
    args.append(nc.dram_tensor("o_scratch", (NH * 2 * D, T), F32, kind="Internal").ap())
    args.append(nc.dram_tensor("r_scratch", (NH, T), F32, kind="Internal").ap())
    layer_kernel(nc, *args)
    r = run_bass_kernel_spmd(nc, [arrays], core_ids=[0])
    return r.results[0]["out"].reshape(1, T, H)
```

```python
from contextlib import ExitStack

import concourse.bass as bass
from concourse import mybir

F32 = mybir.dt.float32
F16 = mybir.dt.float16
BF16 = mybir.dt.bfloat16
U8 = mybir.dt.uint8
ALU = mybir.AluOpType
ACT = mybir.ActivationFunctionType
AX = mybir.AxisListType
RMAX = bass.bass_isa.ReduceOp.max

P = 128
D = 16
EPS = 1e-5
SMALL = 1e-8
HUGE = 1e6
VTOP = 16384.0
TINY = 1e-30


def layer_kernel(nc, x, wq, wk, wv, wo, sq, sk, sv, so, gate, up, down, sg, su, sd, out,
                 q_scratch, k_scratch, o_scratch, r_scratch):
    T, H = x.shape
    HC = H // P
    TT = T // P
    HALF = T // 2
    NH, NKV = wq.shape[1] // D, wk.shape[1] // D
    KV = NKV * D
    REP = NH // NKV
    FT = gate.shape[0]
    QT = NH * D // P
    HPT = P // D
    TERMS = 6
    KROWS = TERMS * D
    SROWS = KROWS + 3
    UNITS = REP * HALF // P
    NQKV = (NH + 2 * NKV) * D
    SCALE = float(D) ** -0.5
    NG = NKV
    NP = NG // 2
    STEPS = 2 * TT
    FU = 2 * FT

    assert KV == P and HC * P == H and QT * P == NH * D and TT % 4 == 0

    K_, V_ = "k", "v"
    PROJ = [K_, 0, V_] + list(range(1, QT))
    order = ("P0 F0 S0 E0 P1 G0 S1 X0 F1 Y0 E1 G1 P2 F2 X1 E2 F3 Y1 G2 P3 F4 E3 V2 G3 "
             "F5 X3 P4 F6 Y3 E4 G4 F7 X4 P5 F8 E5 Y4 F9 G5 F10 X5 F11 Y5 F12")
    order = [(step[0], int(step[1:])) for step in order.split()]
    first = 13
    before, T_AT = 0, 22
    for w in range(first, FU):
        order += [("F", w)]
        if w == T_AT:
            assert before >= UNITS
            order += [("T", 0)]
        until = -(-2 * UNITS * (w + 1 - first) // (FU - first))
        order += [("A", n) for n in range(before, until)]
        before = until
    VY = PROJ.index(V_) % 2
    assert before == 2 * UNITS and len(PROJ) == 6

    NORM = [(t, 0, T) for t in range(QT - 1)] + [(QT - 1, 0, HALF), (QT - 1, HALF, HALF)]
    NU = len(NORM)
    O_INVERT, O_NORM, O_SPLIT = [1, 9, 17], [6, 14, 22], [7, 15, 23]
    D_OUT = [20, 24, 28]
    FILL = 4
    FILLS = [(i, f, part) for i in range(FILL) for f in range(FT) for part in range(2)]
    DBANK = [0, 1, 2, 3, 4, 5, 7, 6]
    tail = [("O", 0), ("D", 4), ("O", 1), ("D", 5), ("O", 2), ("D", 6), ("O", 3), ("D", 7)] + [("O", i) for i in range(4, 8)]

    def at(gp, s):
        gp = gp + s // (2 * STEPS)
        s = s % (2 * STEPS)
        return gp, s // STEPS, s % STEPS // TT, s % TT

    with ExitStack() as ctx:
        def sb(name, shape, dt):
            return ctx.enter_context(nc.sbuf_tensor(name, shape, dt))

        def sem(name):
            return ctx.enter_context(nc.semaphore(name))

        ps = ctx.enter_context(nc.psum_tensor("ps", [P, 8, 512], F32))

        def bank_pair(r):
            return ps[:, 2 * r:2 * r + 2, :].rearrange("p b n -> p (b n)")

        ident = sb("ident", [P, P], F32)
        ones = sb("ones", [P, P], F32)
        eps = sb("eps", [P, 1], F32)
        warm = sb("warm", [P, 1], F32)
        stats = sb("stats", [P, 2, 6], F32)
        mv = sb("mv", [P, TT, 2], F32)
        std = sb("std", [P, TT], F32)
        rstd = sb("rstd", [P, TT], F32)
        room1 = sb("room1", [P, HC * (NQKV + H)], F32)
        wt = room1[:, 0:HC * NQKV].rearrange("p (c n) -> p c n", c=HC)
        wot = room1[:, HC * NQKV:].rearrange("p (c n) -> p c n", c=HC)
        room2 = sb("room2", [P, 2 * REP * HALF], F32)
        xp = room2[:, :].bitcast(F16).rearrange("p (a c n) -> p a c n", a=2, c=HC)
        xhi, xlo = xp[:, 0], xp[:, 1]
        probs = room2[:, :].rearrange("p (b r n) -> p b r n", b=2, r=REP)
        att = room2[:, 0:2 * H].rearrange("p (b n) -> p b n", b=2)
        room3 = sb("room3", [P, 6 * HALF], F32)
        xn = room3[:, 4 * H:6 * H].rearrange("p (b n) -> p b n", b=2)
        th = room3[:, 0:2 * HALF].rearrange("p (b n) -> p b n", b=2)
        gt = room3[:, 2 * HALF:4 * HALF].rearrange("p (b n) -> p b n", b=2)
        hb = room3[:, 4 * HALF:6 * HALF].rearrange("p (b n) -> p b n", b=2)
        oparts = room1[:, 0:QT * T].bitcast(F16).rearrange("p (t a n) -> p t a n", t=QT, a=2)

        sgn = sb("sgn", [P, HC, NQKV], F16)
        sgno = sb("sgno", [P, HC, H], F16)
        scqk = sb("scqk", [P, QT + 1], F32)
        cqk = sb("cqk", [P, QT + 1], F32)
        svb = sb("svb", [P, KV], F32)
        sob = sb("sob", [P, H], F32)
        dsb = sb("dsb", [P, H], F32)
        gsc = sb("gsc", [P, FT], F32)
        usc = sb("usc", [P, FT], F32)
        vg = sb("vg", [P, 4], F32)
        gain = sb("gain", [P, 4], F32)
        wf = sb("wf", [P, 2, 2, HC * P], F16)
        wd = sb("wd", [P, FT, H], F16)
        ffn = [room3[:, i * H:(i + 1) * H] for i in range(6)]
        ffn += [wf[:, :, :, :].rearrange("p a z n -> p (a z n)").bitcast(F32)[:, i * H:(i + 1) * H] for i in range(2)]
        hhi = sb("hhi", [P, FT, T], F16)
        hlo = sb("hlo", [P, FT, T], F16)
        xin = hlo[:, :, :].rearrange("p f n -> p (f n)").bitcast(F32)[:, 0:TT * H].rearrange("p (i n) -> p i n", i=TT)
        y = sb("y", [P, 2, T], F32)
        ga = sb("ga", [P, T], F32)
        gr = sb("gr", [P, T], F32)
        gb = sb("gb", [P, T], U8)
        parts = sb("parts", [P, 3, T], BF16)
        res = parts[:, :, :].rearrange("p a n -> p (a n)").bitcast(F32).rearrange("p (b n) -> p b n", b=3)
        qst = sb("qst", [P, 2, 2, REP, HALF], BF16)
        kA = sb("kA", [P, 2, T], BF16)
        kB = sb("kB", [P, 2, T], BF16)
        vext = sb("vext", [P, TT, NKV, 2 * D], F32)
        vcur = sb("vcur", [P, 2, TT, 2 * D], F32)
        scrap = vcur[:, :, :, :].rearrange("p g k d -> p (g k d)")
        osb = sb("osb", [P, 2, HALF], F32)
        nmx = sb("nmx", [P, 2, UNITS], F32)
        shr = sb("shr", [UNITS, P], F32)
        shp = sb("shp", [UNITS, 2, 3, P], BF16)
        rsum = sb("rsum", [P, QT + 1, T // D], F32)

        x_loaded = [sem(f"x_loaded{i}") for i in range(TT)]
        qkv_loaded = sem("qkv_loaded")
        wo_loaded = sem("wo_loaded")
        vec_loaded = sem("vec_loaded")
        consts_ready = sem("consts_ready")
        kones_ready = sem("kones_ready")
        eps_ready = sem("eps_ready")
        pool_step = sem("pool_step")
        ln_step = sem("ln_step")
        stats_ready = sem("stats_ready")
        std_ready = sem("std_ready")
        xn_ready = sem("xn_ready")
        xT_ready = sem("xT_ready")
        xhi_ready = sem("xhi_ready")
        xlo_ready = sem("xlo_ready")
        sign_ready = sem("sign_ready")
        mag_ready = sem("mag_ready")
        sums_ready = sem("sums_ready")
        factor_step = sem("factor_step")
        factors_ready = sem("factors_ready")
        gain_ready = sem("gain_ready")
        gmax_ready = sem("gmax_ready")
        proj_ready = sem("proj_ready")
        y_ready = sem("y_ready")
        guard_step = sem("guard_step")
        guarded = sem("guarded")
        hi_ready = sem("hi_ready")
        rest_ready = sem("rest_ready")
        mid_ready = sem("mid_ready")
        split_done = sem("split_done")
        k_stored = sem("k_stored")
        q_stored = sem("q_stored")
        vext_ready = sem("vext_ready")
        vcur_ready = sem("vcur_ready")
        wf_loaded = [sem(f"wf_loaded{i}") for i in range(2)]
        wd_loaded = sem("wd_loaded")
        gate_ready = sem("gate_ready")
        up_ready = sem("up_ready")
        th_ready = sem("th_ready")
        gt_ready = sem("gt_ready")
        h_ready = sem("h_ready")
        hhi_ready = sem("hhi_ready")
        hlo_ready = sem("hlo_ready")
        q_loaded = [[sem(f"q_loaded{a}{b}") for b in range(2)] for a in range(2)]
        kA_loaded = [sem(f"kA_loaded{a}") for a in range(2)]
        kB_loaded = [sem(f"kB_loaded{a}") for a in range(2)]
        shift_loaded = [[sem(f"shift_loaded{a}{b}") for b in range(2)] for a in range(2)]
        rows_ready = sem("rows_ready")
        rows_free = sem("rows_free")
        maxT_ready = sem("maxT_ready")
        maxT_free = sem("maxT_free")
        shift_step = sem("shift_step")
        shift_ready = sem("shift_ready")
        scores_ready = sem("scores_ready")
        scores_free = sem("scores_free")
        probs_free = sem("probs_free")
        pv_free = sem("pv_free")
        osb_free = [sem(f"osb_free{i}") for i in range(2)]
        sums_loaded = [sem(f"sums_loaded{u}") for u in range(NU)]
        rsum_ready = sem("rsum_ready")
        rsum_stored = [sem(f"rsum_stored{u}") for u in range(NU)]
        num_loaded = [sem(f"num_loaded{u}") for u in range(NU)]
        rec_loaded = [sem(f"rec_loaded{u}") for u in range(NU)]
        vmax_ready = sem("vmax_ready")
        vred_ready = sem("vred_ready")
        vscale_ready = sem("vscale_ready")
        normed = sem("normed")
        o_hi = sem("o_hi")
        o_split = sem("o_split")
        down_ready = sem("down_ready")
        oproj_ready = sem("oproj_ready")
        att_ready = sem("att_ready")
        ff_ready = sem("ff_ready")
        res_loaded = [sem(f"res_loaded{i}") for i in range(3)]
        res_added = sem("res_added")
        out_ready = sem("out_ready")
        out_stored = sem("out_stored")

        def normalize_io(eng, u):
            t, c0, n = NORM[u]
            for hf in range((c0 + n) // HALF):
                eng.wait_ge(osb_free[hf], 16 * (2 * t + 3))
            heads = o_scratch.rearrange("(h z d) n -> h z d n", z=2, d=D)[t * HPT:(t + 1) * HPT]
            eng.dma_start(rsum[:, u, 0:n // D],
                          heads[:, 1, 0, c0:c0 + n].rearrange("h (b n) -> h b n", b=D)).then_inc(sums_loaded[u], 16)
            if t >= 2:
                eng.wait_ge(o_split, t - 1)
            eng.dma_start(y[:, t % 2, c0:c0 + n], heads[:, 0, :, c0:c0 + n]).then_inc(num_loaded[u], 16)
            eng.wait_ge(rsum_ready, u + 1)
            rec = r_scratch[t * HPT:(t + 1) * HPT, c0:c0 + n]
            eng.dma_start(rec.rearrange("h (b n) -> h b n", b=D), rsum[:, u, 0:n // D]).then_inc(rsum_stored[u], 16)
            eng.wait_ge(rsum_stored[u], 16)
            if t >= 1:
                eng.wait_ge(normed, t)
            eng.dma_start(ga[:, c0:c0 + n], rec.unsqueeze(1).to_broadcast([HPT, D, n])).then_inc(rec_loaded[u], 16)

        x_v = x.rearrange("(i p) h -> i p h", p=P)
        block = ctx.enter_context(nc.Block())

        @block.sync
        def _(sp):
            def load_queries(g, par, hf):
                src = q_scratch[bass.ds(g * REP, REP), :, :, hf * HALF:(hf + 1) * HALF]
                row = 0
                for n in (3, 2, 1):
                    sp.dma_start(qst[row:row + n * D, par, hf],
                                 src[:, 3 - n:3].rearrange("h t d n -> (t d) h n")).then_inc(q_loaded[par][hf], 16)
                    row += n * D

            def load_keys(buf, loaded, g, par):
                sp.dma_start(buf[0:KROWS, par, :],
                             k_scratch[bass.ds(g, 1)].rearrange("g t d n -> (g t d) n")).then_inc(loaded[par], 16)

            def load_shift(v, par, hf):
                sp.wait_ge(shift_ready, v + 1)
                for part in range(3):
                    dst = qst[KROWS + part:KROWS + part + 1, par, hf].rearrange("p h n -> p (h n)")
                    sp.dma_start(dst, shp[:, hf, part, :]).then_inc(shift_loaded[par][hf], 16)

            def load_weights(w_, c0):
                sp.dma_start(wt[:, :, c0:c0 + w_.shape[1]],
                             w_.rearrange("(c p) o -> p c o", p=P)).then_inc(qkv_loaded, 16)

            sp.sem_inc(rows_free, 2)
            sp.sem_inc(maxT_free, 1)
            sp.sem_inc(scores_free, 2)
            sp.sem_inc(probs_free, 2)
            sp.sem_inc(pv_free, 1)
            for b in range(2):
                sp.sem_inc(osb_free[b], 16)

            for i in range(TT):
                sp.dma_start(xin[:, i, :], x_v[i]).then_inc(x_loaded[i], 16)
                if i == TT // 2:
                    load_weights(wk, NH * D)
            load_weights(wq, 0)
            load_weights(wv, NH * D + KV)
            sp.dma_start(wot[:, :, :], wo.rearrange("(c p) o -> p c o", p=P)).then_inc(wo_loaded, 16)

            splits = 0
            for what in PROJ:
                if what == V_:
                    continue
                splits += 1
                sp.wait_ge(mid_ready, splits)
                sp.wait_ge(split_done, splits)
                if what == K_:
                    for term, part in enumerate([0, 1, 2, 0, 1, 0]):
                        sp.dma_start(k_scratch[:, term], parts[:, part, :]).then_inc(k_stored, 16)
                    sp.wait_ge(k_stored, 16 * TERMS)
                    for par in range(2):
                        load_keys(kA, kA_loaded, par, par)
                        load_keys(kB, kB_loaded, par, par)
                else:
                    for part in range(3):
                        sp.dma_start(q_scratch[what * HPT:(what + 1) * HPT, 2 - part], parts[:, part, :]).then_inc(q_stored, 16)
                    if what == 0:
                        sp.wait_ge(q_stored, 48)
                        for g in range(2):
                            for hf in range(2):
                                load_queries(g, g, hf)
            sp.wait_ge(q_stored, 48 * QT)
            load_shift(0, 0, 0)

            def half_ended(gp, s, last):
                _, par, hf, _ = at(gp, s - 1)
                v = gp * 4 + s // TT - 1
                g = gp * 2 + par
                if not last:
                    sp.wait_ge(scores_ready, (v + 1) * REP * TT)
                    load_queries(g + 2, par, hf)
                    if hf == 0:
                        sp.wait_ge(rows_ready, (g + 1) * 2 * UNITS)
                        load_keys(kA, kA_loaded, g + 2, par)
                    else:
                        load_keys(kB, kB_loaded, g + 2, par)
                if not last or par == 0:
                    load_shift(v + 2, 1 - par, hf)
                sp.wait_ge(pv_free, v + 2)
                sp.dma_start(o_scratch[bass.ds(g * (REP * 2 * D), REP * 2 * D), hf * HALF:(hf + 1) * HALF],
                             osb[:, hf, :]).then_inc(osb_free[hf], 16)

            load_shift(1, 0, 1)
            for gp in range(NP - 1):
                for s in range(TT, 2 * STEPS + 1, TT):
                    half_ended(gp, s, False)

            for s in range(TT, 2 * STEPS + 1, TT):
                half_ended(NP - 1, s, True)
                if s >= STEPS + TT:
                    normalize_io(sp, QT - 1 + (s - STEPS - TT) // TT)
            for kind, i in tail:
                if kind == "O":
                    sp.wait_ge(out_ready, i + 1)
                    sp.dma_start(out.rearrange("(i p) h -> i p h", p=P)[i], ffn[i]).then_inc(out_stored, 16)
            sp.wait_ge(out_stored, 16 * TT)

        @block.gpsimd
        def _(pool):
            def add_residual(i):
                pool.wait_ge(ff_ready, i + 1)
                pool.wait_ge(res_loaded[i % 3], 16 * (i // 3 + 1))
                nc.gpsimd.tensor_tensor(ffn[i], ffn[i], res[:, i % 3, :], ALU.add).then_inc(res_added, 1)

            def load_ffn(f):
                pool.dma_start(wf[:, f % 2, 0, :], gate[f]).then_inc(wf_loaded[f % 2], 16)
                pool.dma_start(wf[:, f % 2, 1, :], up[f]).then_inc(wf_loaded[f % 2], 16)

            nc.gpsimd.memset(ident[:, :], 0.0).then_inc(pool_step, 1)
            pool.wait_ge(pool_step, 1)
            nc.gpsimd.affine_select(out=ident[:, :], in_=ident[:, :], compare_op=ALU.not_equal, fill=1.0, base=0,
                                    pattern=[[-1, P]], channel_multiplier=1).then_inc(consts_ready, 1)
            nc.gpsimd.memset(ones[:, :], 1.0).then_inc(consts_ready, 1)
            load_ffn(0)
            load_ffn(1)
            nc.gpsimd.memset(vext[:, :, :, :], 1.0).then_inc(consts_ready, 1)
            pool.wait_ge(gain_ready, 1)
            nc.gpsimd.partition_all_reduce(gain[:, 1:2], gain[:, 0:1], P, RMAX).then_inc(gmax_ready, 1)

            def hidden_low(w):
                f, hf = w // 2, w % 2
                pool.wait_ge(hhi_ready, w + 1)
                nc.gpsimd.tensor_tensor(hlo[:, f, hf * HALF:(hf + 1) * HALF], hb[:, w % 2, :],
                                        hhi[:, f, hf * HALF:(hf + 1) * HALF], ALU.subtract).then_inc(hlo_ready, 1)

            for kind, w in order:
                if kind == "V":
                    pool.wait_ge(vmax_ready, 1)
                    nc.gpsimd.partition_all_reduce(vg[:, 1:2], vg[:, 0:1], P, RMAX).then_inc(vred_ready, 1)
                if kind != "F":
                    continue
                f, hf = w // 2, w % 2
                if hf == 0 and 1 <= f < FT - 1:
                    pool.wait_ge(up_ready, w)
                    load_ffn(f + 1)
                if w == 3:
                    pool.dma_start(wd[:, :, :], down.rearrange("(f p) h -> p f h", p=P)).then_inc(wd_loaded, 16)
                if w >= 1:
                    hidden_low(w - 1)
            hidden_low(FU - 1)
            pool.wait_ge(vext_ready, 1)
            for g in range(2):
                nc.gpsimd.tensor_copy(vcur[:, g, :, :], vext[:, :, g, :]).then_inc(vcur_ready, 1)
            for g in range(2, NG):
                pool.wait_ge(probs_free, 2 + STEPS * (g - 1))
                nc.gpsimd.tensor_copy(vcur[:, g % 2, :, :], vext[:, :, g, :]).then_inc(vcur_ready, 1)
            for u in range(QT - 1):
                normalize_io(pool, u)
            for i in range(TT):
                if i >= 3:
                    pool.wait_ge(res_added, i - 2)
                pool.dma_start(res[:, i % 3, :], x_v[i]).then_inc(res_loaded[i % 3], 16)
                if i >= 2:
                    add_residual(i - 2)
            for i in range(TT - 2, TT):
                add_residual(i)

        @block.scalar
        def _(act):
            act.wait_ge(eps_ready, 1)
            nc.scalar.activation(warm[:, :], eps[:, :], ACT.Sqrt)
            act.dma_start(scqk[:, 0:QT], sq).then_inc(vec_loaded, 16)
            act.dma_start(scqk[:, QT:QT + 1], sk).then_inc(vec_loaded, 16)
            act.dma_start(svb[:, :], sv.to_broadcast([P, KV])).then_inc(vec_loaded, 16)
            act.dma_start(sob[:, :], so.to_broadcast([P, H])).then_inc(vec_loaded, 16)
            act.dma_start(dsb[:, :], sd.to_broadcast([P, H])).then_inc(vec_loaded, 16)
            act.dma_start(gsc[:, :], sg).then_inc(vec_loaded, 16)
            act.dma_start(usc[:, :], su).then_inc(vec_loaded, 16)
            def xhi_copy(i):
                act.wait_ge(xT_ready, i + 1)
                nc.scalar.copy(xhi[:, :, i * P:(i + 1) * P],
                               ps[:, i % 4, :].rearrange("p (c n) -> p c n", c=HC)).then_inc(xhi_ready, 1)

            for i in range(TT):
                act.wait_ge(stats_ready, i + 1)
                nc.scalar.activation(std[:, i:i + 1], mv[:, i, 1:2], ACT.Sqrt, bias=eps[:, 0:1]).then_inc(std_ready, 1)
                if i >= 1:
                    xhi_copy(i - 1)
            xhi_copy(TT - 1)
            act.wait_ge(qkv_loaded, 48)
            for c0, c1 in ((NH * D, NQKV), (0, NH * D)):
                nc.scalar.activation(sgn[:, :, c0:c1], wt[:, :, c0:c1], ACT.Sign).then_inc(sign_ready, 1)
            act.wait_ge(sign_ready, 2)
            nc.scalar.activation(wt, wt, ACT.Abs).then_inc(mag_ready, 1)
            act.wait_ge(wo_loaded, 16)
            nc.scalar.activation(sgno[:, :, :], wot, ACT.Sign).then_inc(sign_ready, 1)
            act.wait_ge(sign_ready, 3)
            nc.scalar.activation(wot, wot, ACT.Abs).then_inc(mag_ready, 1)

            def hidden_high(n):
                f, hf = n // 2, n % 2
                act.wait_ge(h_ready, n + 1)
                nc.scalar.copy(hhi[:, f, hf * HALF:(hf + 1) * HALF], hb[:, n % 2, :]).then_inc(hhi_ready, 1)

            splits = 0
            for kind, n in order:
                if kind == "E" and PROJ[n] != V_:
                    col = QT if PROJ[n] == K_ else PROJ[n]
                    act.wait_ge(proj_ready, n + 1)
                    act.wait_ge(factors_ready, 2)
                    if n >= 2:
                        act.wait_ge(split_done, sum(1 for m in PROJ[:n - 1] if m != V_))
                        act.wait_ge(guarded, n - 1)
                        if PROJ[n - 2] == V_:
                            act.wait_ge(vext_ready, 1)
                    nc.scalar.activation(y[:, n % 2, :], bank_pair(n % 2), ACT.Copy,
                                         scale=cqk[:, col:col + 1]).then_inc(y_ready, 1)
                elif kind == "V":
                    act.wait_ge(vscale_ready, 1)
                    act.wait_ge(consts_ready, 3)
                    nc.scalar.activation(vext[:, :, :, 0:D].rearrange("p k g d -> p (k g) d"),
                                         y[:, VY, :].rearrange("p (m d) -> p m d", d=D), ACT.Copy,
                                         scale=vg[:, 3:4]).then_inc(vext_ready, 1)
                elif kind == "X":
                    splits += 1
                    act.wait_ge(guarded, n + 1)
                    if splits == 2:
                        act.wait_ge(k_stored, 16 * TERMS)
                    elif splits > 2:
                        act.wait_ge(q_stored, 48 * (splits - 2))
                    nc.scalar.copy(parts[:, 0, :], y[:, n % 2, :]).then_inc(hi_ready, 1)
                elif kind == "Y":
                    act.wait_ge(rest_ready, splits)
                    nc.scalar.copy(parts[:, 1, :], gr[:, :]).then_inc(mid_ready, 1)
                elif kind == "F":
                    f = n // 2
                    if n >= 1:
                        hidden_high(n - 1)
                    act.wait_ge(gate_ready, n + 1)
                    if n == 0:
                        act.wait_ge(factors_ready, 1)
                    if n >= 2:
                        act.wait_ge(gt_ready, n - 1)
                    nc.scalar.activation(th[:, n % 2, :], ps[:, 4 + 2 * (n % 2), :], ACT.Tanh,
                                         scale=gsc[:, f:f + 1]).then_inc(th_ready, 1)
            hidden_high(FU - 1)

            def exps(gp, s):
                _, _, _, kt = at(gp, s)
                step = gp * (2 * STEPS) + s
                act.wait_ge(probs_free, step + 1)
                for r in range(REP):
                    act.wait_ge(scores_ready, step * REP + r + 1)
                    nc.scalar.activation(probs[:, s % 2, r, :], ps[:, 4 + r % 2, :], ACT.Exp,
                                         scale=SCALE).then_inc(scores_free, 1)

            def take_output(gp, s):
                _, par, hf, _ = at(gp, s - 1)
                v = gp * 4 + s // TT - 1
                act.wait_ge(probs_free, (v + 1) * TT + 2)
                act.wait_ge(osb_free[hf], 16 * (gp * 2 + par + 1))
                nc.scalar.copy(osb[:, hf, :], ps[:, 6, :]).then_inc(pv_free, 1)

            def o_high(u):
                t, c0, n = NORM[u]
                act.wait_ge(normed, u + 1)
                nc.scalar.copy(oparts[:, t, 0, c0:c0 + n], y[:, t % 2, c0:c0 + n]).then_inc(o_hi, 1)

            act.wait_ge(up_ready, FU)
            exps(0, 0)
            for gp in range(NP):
                for s in range(1, 2 * STEPS + 1):
                    if not (gp == NP - 1 and s == 2 * STEPS):
                        exps(gp, s)
                    if s % TT == 0:
                        take_output(gp, s)
                    if gp == NP - 1 and s in O_SPLIT:
                        o_high(O_SPLIT.index(s))
            for u in range(len(O_SPLIT), NU):
                o_high(u)

        @block.vector
        def _(dve):
            nc.vector.memset(eps[:, :], EPS).then_inc(eps_ready, 1)
            nc.vector.memset(kB[KROWS:P, :, :], 1.0).then_inc(kones_ready, 1)

            ln = 0

            def x_stats(i):
                nonlocal ln
                dve.wait_ge(x_loaded[i], 16)
                nc.vector.bn_stats(stats[:, i % 2, :], xin[:, i, :]).then_inc(ln_step, 1)
                ln += 1
                dve.wait_ge(ln_step, ln)
                nc.vector.bn_aggr(mv[:, i, :], stats[:, i % 2, :]).then_inc(stats_ready, 1)

            def normalize(i):
                nonlocal ln
                dve.wait_ge(std_ready, i + 1)
                nc.vector.reciprocal(rstd[:, i:i + 1], std[:, i:i + 1]).then_inc(ln_step, 1)
                ln += 1
                dve.wait_ge(ln_step, ln)
                if i >= 2:
                    dve.wait_ge(xT_ready, i - 1)
                nc.vector.tensor_scalar(xn[:, i % 2, :], xin[:, i, :], mv[:, i, 0:1], rstd[:, i:i + 1],
                                        ALU.subtract, ALU.mult).then_inc(xn_ready, 1)

            def x_low(i):
                dve.wait_ge(xhi_ready, i + 1)
                nc.vector.tensor_tensor(xlo[:, :, i * P:(i + 1) * P],
                                        ps[:, i % 4, :].rearrange("p (c n) -> p c n", c=HC),
                                        xhi[:, :, i * P:(i + 1) * P], ALU.subtract).then_inc(xlo_ready, 1)

            x_stats(0)
            x_stats(1)
            for i in range(TT + 2):
                if i < TT:
                    normalize(i)
                if i + 2 < TT:
                    x_stats(i + 2)
                if i >= 2:
                    x_low(i - 2)

            steps = 0

            def step(ins):
                nonlocal steps
                steps += 1
                ins.then_inc(factor_step, 1)
                dve.wait_ge(factor_step, steps)

            dve.wait_ge(vec_loaded, 16 * 7)
            step(nc.vector.tensor_tensor(usc[:, :], usc[:, :], gsc[:, :], ALU.mult))
            nc.vector.tensor_reduce(gain[:, 0:1], usc[:, :], AX.X, ALU.max, apply_absolute_value=True).then_inc(gain_ready, 1)
            step(nc.vector.tensor_scalar(gsc[:, :], gsc[:, :], 0.5, None, ALU.mult))
            dve.wait_ge(gmax_ready, 1)
            step(nc.vector.tensor_scalar(gain[:, 2:3], gain[:, 1:2], 8.0, 1e-30, ALU.mult, ALU.max))
            step(nc.vector.reciprocal(gain[:, 3:4], gain[:, 2:3]))
            step(nc.vector.tensor_scalar(usc[:, :], usc[:, :], gain[:, 3:4], 0.5, ALU.mult, ALU.mult))
            nc.vector.tensor_scalar(dsb[:, :], dsb[:, :], gain[:, 2:3], None, ALU.mult).then_inc(factors_ready, 1)

            guards = 0

            def guard(v_, n_):
                nonlocal guards
                mask, repl, less = gb[:, 0:n_], ga[:, 0:n_], gr[:, 0:n_]
                nc.vector.tensor_scalar(repl, v_, 0.0, HUGE, ALU.is_gt, ALU.mult).then_inc(guard_step, 1)
                nc.vector.tensor_scalar(less, v_, 0.0, HUGE, ALU.is_lt, ALU.mult).then_inc(guard_step, 1)
                nc.vector.tensor_scalar(mask, v_, 0.0, 0.0, ALU.mult, ALU.not_equal).then_inc(guard_step, 1)
                dve.wait_ge(guard_step, guards + 2)
                nc.vector.tensor_tensor(repl, repl, less, ALU.subtract).then_inc(guard_step, 1)
                guards += 4
                dve.wait_ge(guard_step, guards)
                return nc.vector.copy_predicated(v_, mask, repl)

            def row_max(n, hf, idx):
                dve.wait_ge(rows_ready, n + 1)
                nc.vector.tensor_reduce(nmx[:, hf, idx:idx + 1], bank_pair(idx % 2), AX.X, ALU.max,
                                        negate=True).then_inc(rows_free, 1)

            def split_max(v, hf):
                dve.wait_ge(maxT_ready, v + 1)
                nc.vector.tensor_copy(shp[:, hf, 0, :], ps[0:UNITS, 7, 0:P]).then_inc(shift_step, 1)
                dve.wait_ge(shift_step, 2 * v + 1)
                nc.vector.tensor_tensor(shr[:, :], ps[0:UNITS, 7, 0:P], shp[:, hf, 0, :], ALU.subtract).then_inc(maxT_free, 1)
                dve.wait_ge(maxT_free, v + 2)
                nc.vector.tensor_copy(shp[:, hf, 1, :], shr[:, :]).then_inc(shift_step, 1)
                dve.wait_ge(shift_step, 2 * v + 2)
                nc.vector.tensor_tensor(shp[:, hf, 2, :], shr[:, :], shp[:, hf, 1, :], ALU.subtract).then_inc(shift_ready, 1)

            splits = 0
            for kind, n in order:
                if kind == "E" and PROJ[n] == V_:
                    dve.wait_ge(proj_ready, n + 1)
                    dve.wait_ge(factors_ready, 3)
                    dve.wait_ge(mid_ready, splits)
                    nc.vector.tensor_tensor(y[:, n % 2, :].rearrange("p (k m) -> p k m", m=KV),
                                            bank_pair(n % 2).rearrange("p (k m) -> p k m", m=KV),
                                            svb[:, :].unsqueeze(1).to_broadcast([P, TT, KV]),
                                            ALU.mult).then_inc(y_ready, 1)
                elif kind == "S" and n == 0:
                    dve.wait_ge(sums_ready, 1)
                    step(nc.vector.tensor_scalar(cqk[:, :], ps[:, 7, 0:QT + 1], 1.0 / H, SMALL, ALU.mult, ALU.max))
                    nc.vector.tensor_tensor(cqk[:, :], cqk[:, :], scqk[:, :], ALU.mult).then_inc(factors_ready, 1)
                    step(nc.vector.tensor_scalar(ga[:, 0:KV], ps[:, 7, KV:2 * KV], 1.0 / H, SMALL, ALU.mult, ALU.max))
                    nc.vector.tensor_tensor(svb[:, :], ga[:, 0:KV], svb[:, :], ALU.mult).then_inc(factors_ready, 1)
                elif kind == "S":
                    dve.wait_ge(sums_ready, 2)
                    step(nc.vector.tensor_scalar(scrap, ps[:, 6, :], 1.0 / H, SMALL, ALU.mult, ALU.max))
                    nc.vector.tensor_tensor(sob[:, :], scrap, sob[:, :], ALU.mult).then_inc(factors_ready, 1)
                elif kind == "G":
                    dve.wait_ge(y_ready, n + 1)
                    if n == 0:
                        dve.wait_ge(factors_ready, 3)
                    else:
                        dve.wait_ge(guarded, n)
                        dve.wait_ge(split_done, splits)
                    guard(y[:, n % 2, :], T).then_inc(guarded, 1)
                    if PROJ[n] == V_:
                        dve.wait_ge(guarded, n + 1)
                        nc.vector.tensor_reduce(vg[:, 0:1], y[:, n % 2, :], AX.X, ALU.max,
                                                apply_absolute_value=True).then_inc(vmax_ready, 1)
                elif kind == "X":
                    splits += 1
                    dve.wait_ge(hi_ready, splits)
                    nc.vector.tensor_tensor(gr[:, :], y[:, n % 2, :], parts[:, 0, :], ALU.subtract).then_inc(rest_ready, 1)
                elif kind == "Y":
                    dve.wait_ge(mid_ready, splits)
                    nc.vector.tensor_tensor(parts[:, 2, :], gr[:, :], parts[:, 1, :], ALU.subtract).then_inc(split_done, 1)
                elif kind == "F":
                    f, hf = n // 2, n % 2
                    dve.wait_ge(th_ready, n + 1)
                    nc.vector.scalar_tensor_tensor(out=gt[:, n % 2, :], in0=th[:, n % 2, :], scalar=1.0,
                                                   in1=ps[:, 4 + 2 * (n % 2), :], op0=ALU.add,
                                                   op1=ALU.mult).then_inc(gt_ready, 1)
                    dve.wait_ge(gt_ready, n + 1)
                    dve.wait_ge(up_ready, n + 1)
                    if n >= 2:
                        dve.wait_ge(hlo_ready, n - 1)
                    nc.vector.scalar_tensor_tensor(out=hb[:, n % 2, :], in0=ps[:, 5 + 2 * (n % 2), :],
                                                   scalar=usc[:, f:f + 1], in1=gt[:, n % 2, :],
                                                   op0=ALU.mult, op1=ALU.mult).then_inc(h_ready, 1)
                elif kind == "V":
                    dve.wait_ge(vred_ready, 1)
                    step(nc.vector.tensor_scalar(vg[:, 2:3], vg[:, 1:2], TINY, 1.0 / VTOP, ALU.max, ALU.mult))
                    nc.vector.reciprocal(vg[:, 3:4], vg[:, 2:3]).then_inc(vscale_ready, 1)
                    nc.vector.tensor_scalar(sob[:, :], sob[:, :], vg[:, 2:3], None, ALU.mult).then_inc(vscale_ready, 1)
                elif kind == "A":
                    row_max(n, n // UNITS, n % UNITS)
                elif kind == "T":
                    split_max(0, 0)

            def step_rows(gp, s, last):
                gp_, par, hf, kt = at(gp, s)
                if not (last and (par == 1 or s == 2 * STEPS)):
                    ga_ = gp_ * 2 + par + 1
                    for j in range(2):
                        idx = 2 * kt + j
                        row_max(ga_ * (2 * UNITS) + hf * UNITS + idx, hf, idx)
                if s % TT == 0 and not (last and s >= STEPS + TT):
                    v = gp * 4 + s // TT + 1
                    if s > 0:
                        _, ppar, phf, _ = at(gp, s - 1)
                        dve.wait_ge(shift_loaded[ppar][phf], 48 * (gp + 1))
                    else:
                        phf = 1
                    split_max(v, phf)

            def invert(u):
                dve.wait_ge(sums_loaded[u], 16)
                n = NORM[u][2] // D
                nc.vector.reciprocal(rsum[:, u, 0:n], rsum[:, u, 0:n]).then_inc(rsum_ready, 1)

            def normalize_output(u):
                t, c0, n = NORM[u]
                dve.wait_ge(num_loaded[u], 16)
                dve.wait_ge(rec_loaded[u], 16)
                nc.vector.tensor_tensor(y[:, t % 2, c0:c0 + n], y[:, t % 2, c0:c0 + n], ga[:, c0:c0 + n],
                                        ALU.mult).then_inc(normed, 1)

            def o_low(u):
                t, c0, n = NORM[u]
                dve.wait_ge(o_hi, u + 1)
                nc.vector.tensor_tensor(oparts[:, t, 1, c0:c0 + n], y[:, t % 2, c0:c0 + n], oparts[:, t, 0, c0:c0 + n],
                                        ALU.subtract).then_inc(o_split, 1)

            def down_out(i):
                dve.wait_ge(down_ready, i + 1)
                nc.vector.tensor_tensor(ffn[i], ps[:, DBANK[i], :], dsb[:, :], ALU.mult).then_inc(ff_ready, 1)

            def rows_out(i):
                dve.wait_ge(oproj_ready, i + 1)
                if i >= 2:
                    dve.wait_ge(out_ready, i - 1)
                nc.vector.tensor_tensor(att[:, i % 2, :], ps[:, DBANK[i], :], sob[:, :], ALU.mult).then_inc(att_ready, 1)
                dve.wait_ge(att_ready, 2 * i + 1)
                guard(att[:, i % 2, :], H).then_inc(att_ready, 1)
                dve.wait_ge(att_ready, 2 * i + 2)
                dve.wait_ge(res_added, i + 1)
                nc.vector.tensor_tensor(ffn[i], ffn[i], att[:, i % 2, :], ALU.add).then_inc(out_ready, 1)

            step_rows(0, 0, False)
            for gp in range(NP):
                for s in range(1, 2 * STEPS + 1):
                    if gp == NP - 1 and s == 2 * STEPS:
                        break
                    step_rows(gp, s, gp == NP - 1)
                    if gp == NP - 1:
                        if s in O_INVERT:
                            invert(O_INVERT.index(s))
                        if s in O_NORM:
                            normalize_output(O_NORM.index(s))
                        if s in O_SPLIT:
                            o_low(O_SPLIT.index(s))
                        if s in D_OUT:
                            down_out(D_OUT.index(s))
                            
            invert(QT - 1)
            normalize_output(QT - 1)
            o_low(QT - 1)
            down_out(FILL - 1)
            for n, (kind, i) in enumerate(tail):
                if n == 1:
                    invert(QT)
                    normalize_output(QT)
                    o_low(QT)
                if kind == "D":
                    down_out(i)
                else:
                    rows_out(i)

        @block.tensor
        def _(pe):
            pe.wait_ge(consts_ready, 1)
            for i in range(TT):
                pe.wait_ge(xn_ready, i + 1)
                if i >= 4:
                    pe.wait_ge(xlo_ready, i - 3)
                for c in range(HC):
                    mm = nc.tensor.transpose(ps[:, i % 4, c * P:(c + 1) * P], xn[:, i % 2, c * P:(c + 1) * P], ident[:, :])
                mm.then_inc(xT_ready, 1)

            def sum_magnitudes(part):
                pe.wait_ge(mag_ready, part + 1)
                if part == 0:
                    pe.wait_ge(consts_ready, 2)
                    for col in range(QT + 1):
                        for c in range(HC):
                            nc.tensor.matmul(ps[:, 7, col:col + 1], wt[:, c, col * P:(col + 1) * P], ones[:, 0:1],
                                             start=(c == 0), stop=(c == HC - 1))
                    for c in range(HC):
                        mm = nc.tensor.matmul(ps[:, 7, KV:2 * KV], ones[:, :], wt[:, c, NH * D + KV:NQKV],
                                              start=(c == 0), stop=(c == HC - 1))
                else:
                    for c in range(HC):
                        mm = nc.tensor.matmul(ps[:, 6, :], ones[:, :], wot[:, c, :], start=(c == 0), stop=(c == HC - 1))
                mm.then_inc(sums_ready, 1)

            def project(n):
                what = PROJ[n]
                pe.wait_ge(sign_ready, 1 if n == 0 else 2)
                pe.wait_ge(xlo_ready, TT)
                if n >= 2:
                    pe.wait_ge(y_ready, n - 1)
                if what == V_:
                    for k in range(TT):
                        for c in range(HC):
                            for xs in (xhi, xlo):
                                mm = nc.tensor.matmul(bank_pair(n % 2)[:, k * KV:(k + 1) * KV], xs[:, c, k * P:(k + 1) * P],
                                                      sgn[:, c, NH * D + KV:NQKV], start=(c == 0 and xs is xhi),
                                                      stop=(c == HC - 1 and xs is xlo))
                else:
                    c0 = NH * D if what == K_ else what * P
                    for hf in range(2):
                        for c in range(HC):
                            for xs in (xhi, xlo):
                                mm = nc.tensor.matmul(ps[:, 2 * (n % 2) + hf, :], sgn[:, c, c0:c0 + P],
                                                      xs[:, c, hf * HALF:(hf + 1) * HALF],
                                                      start=(c == 0 and xs is xhi), stop=(c == HC - 1 and xs is xlo))
                mm.then_inc(proj_ready, 1)

            def feed_forward(w):
                f, hf = w // 2, w % 2
                pe.wait_ge(wf_loaded[f % 2], 32 * (f // 2 + 1))
                if w == 1:
                    pe.wait_ge(factors_ready, 4)
                elif w >= 2:
                    pe.wait_ge(h_ready, w - 1)
                if w == T_AT + 1:
                    pe.wait_ge(maxT_free, 2)
                for z, ready in ((0, gate_ready), (1, up_ready)):
                    for c in range(HC):
                        for xs in (xhi, xlo):
                            mm = nc.tensor.matmul(ps[:, 4 + 2 * (w % 2) + z, :], wf[:, f % 2, z, c * P:(c + 1) * P],
                                                  xs[:, c, hf * HALF:(hf + 1) * HALF],
                                                  start=(c == 0 and xs is xhi), stop=(c == HC - 1 and xs is xlo))
                    mm.then_inc(ready, 1)

            def rows(n, par, hf, idx):
                head, qt = idx // (HALF // P), idx % (HALF // P)
                pe.wait_ge(rows_free, n + 1)
                for b in range(2):
                    mm = nc.tensor.matmul(ps[:, 2 * (idx % 2) + b, :], qst[0:KROWS, par, hf, head, qt * P:(qt + 1) * P],
                                          kA[0:KROWS, par, b * HALF:(b + 1) * HALF], start=True, stop=True)
                mm.then_inc(rows_ready, 1)

            def transpose_max(v, hf):
                if v == 1:
                    pe.wait_ge(h_ready, FU)
                pe.wait_ge(rows_free, 2 + (v + 1) * UNITS)
                pe.wait_ge(maxT_free, v + 1)
                nc.tensor.transpose(ps[0:UNITS, 7, 0:P], nmx[:, hf, :], ident[:, :]).then_inc(maxT_ready, 1)

            for kind, n in order:
                if kind == "P":
                    project(n)
                elif kind == "S":
                    sum_magnitudes(n)
                elif kind == "F":
                    feed_forward(n)
                elif kind == "A":
                    if n == 0:
                        pe.wait_ge(y_ready, len(PROJ))
                        pe.wait_ge(kA_loaded[0], 16)
                    if n % UNITS == 0:
                        pe.wait_ge(q_loaded[0][n // UNITS], 48)
                    rows(n, 0, n // UNITS, n % UNITS)
                elif kind == "T":
                    pe.wait_ge(h_ready, T_AT)
                    transpose_max(0, 0)

            def down_proj(i, f, part):
                bank = DBANK[i]
                if f == 0 and part == 0:
                    if bank < 4:
                        pe.wait_ge(wd_loaded, 16)
                        pe.wait_ge(rows_free, 2 + NG * 2 * UNITS)
                    elif bank < 6:
                        pe.wait_ge(scores_free, 2 + NG * STEPS * REP)
                    elif bank == 6:
                        pe.wait_ge(pv_free, 2 * NG + 1)
                    else:
                        pe.wait_ge(maxT_free, 2 * NG + 1)
                mm = nc.tensor.matmul(ps[:, bank, :], (hhi, hlo)[part][:, f, i * P:(i + 1) * P], wd[:, f, :],
                                      start=(f == 0 and part == 0), stop=(f == FT - 1 and part == 1))
                if f == FT - 1 and part == 1:
                    mm.then_inc(down_ready, 1)

            def scores(gp, s, last):
                gp_, par, hf, kt = at(gp, s)
                step_ = gp * (2 * STEPS) + s
                if kt == 0:
                    pe.wait_ge(q_loaded[par][hf], 48 * (gp_ + 1))
                    pe.wait_ge(shift_loaded[par][hf], 48 * (gp_ + 1))
                    if hf == 0:
                        pe.wait_ge(kB_loaded[par], 16 * (gp_ + 1))
                with_rows = not (last and par == 1)
                if with_rows and kt == 0:
                    pe.wait_ge(q_loaded[1 - par][hf], 48 * (gp_ + par + 1))
                    if hf == 0:
                        pe.wait_ge(kA_loaded[1 - par], 16 * (gp_ + par + 1))
                if not with_rows:
                    fill = list(range(len(FILLS) * (s - STEPS) // STEPS, len(FILLS) * (s - STEPS + 1) // STEPS))
                for r in range(REP):
                    pe.wait_ge(scores_free, step_ * REP + r + 1)
                    nc.tensor.matmul(ps[:, 4 + r % 2, :], kB[0:SROWS, par, kt * P:(kt + 1) * P],
                                     qst[0:SROWS, par, hf, r, :], start=True, stop=True).then_inc(scores_ready, 1)
                    if r == 0 and with_rows:
                        for idx in (2 * kt, 2 * kt + 1):
                            rows((gp_ * 2 + par + 1) * (2 * UNITS) + hf * UNITS + idx, 1 - par, hf, idx)
                    elif r == 0:
                        for n in fill:
                            down_proj(*FILLS[n])
                    elif r == 2 and s > 0:
                        times_values(gp, s - 1)
                if kt == 0 and not (last and s >= STEPS + TT):
                    transpose_max(gp * 4 + s // TT + 1, 1 - hf)

            def times_values(gp, s):
                gp_, par, hf, kt = at(gp, s)
                step_ = gp * (2 * STEPS) + s
                if kt == 0:
                    pe.wait_ge(pv_free, gp * 4 + s // TT + 1)
                    if hf == 0:
                        pe.wait_ge(vcur_ready, gp * 2 + par + 1)
                pe.wait_ge(scores_free, 2 + (step_ + 1) * REP)
                for r in range(REP):
                    mm = nc.tensor.matmul(ps[32 * r:32 * r + 32, 6, :], vcur[:, par, kt, :], probs[:, s % 2, r, :],
                                          start=(kt == 0), stop=(kt == TT - 1))
                mm.then_inc(probs_free, 1)

            pe.wait_ge(h_ready, FU - 1)
            pe.wait_ge(kones_ready, 1)
            scores(0, 0, False)
            for gp in range(NP):
                last = gp == NP - 1
                for s in range(2 * STEPS):
                    if last and s == 2 * STEPS - 1:
                        times_values(gp, s)
                    else:
                        scores(gp, s + 1, last)

            def out_proj(i):
                pe.wait_ge(sign_ready, 3)
                pe.wait_ge(o_split, NU if i >= TT // 2 else NU - 1)
                pe.wait_ge(ff_ready, i + 1)
                for t in range(QT):
                    for part in range(2):
                        mm = nc.tensor.matmul(ps[:, DBANK[i], :], oparts[:, t, part, i * P:(i + 1) * P], sgno[:, t, :],
                                              start=(t == 0 and part == 0), stop=(t == QT - 1 and part == 1))
                mm.then_inc(oproj_ready, 1)

            for kind, i in tail:
                if kind == "O":
                    out_proj(i)
                else:
                    for f in range(FT):
                        for part in range(2):
                            down_proj(i, f, part)


_INS = ["x", "wq", "wk", "wv", "wo", "sq", "sk", "sv", "so", "gate", "up", "down", "sg", "su", "sd"]


def kernel(L0_attn_hidden_states, L0_attn_q_weight, L0_attn_q_scale, L0_attn_k_weight, L0_attn_k_scale,
           L0_attn_v_weight, L0_attn_v_scale, L0_attn_o_weight, L0_attn_o_scale, L0_ffn_gate_t, L0_ffn_up_t,
           L0_ffn_down_t, L0_ffn_gate_s, L0_ffn_up_s, L0_ffn_down_s):
    import numpy as np
    import concourse.bacc as bacc
    from concourse.bass_utils import run_bass_kernel_spmd

    _, T, H = L0_attn_hidden_states.shape
    FT = L0_ffn_gate_t.shape[0] // P

    def columns(v):
        return np.ascontiguousarray(np.asarray(v).reshape(-1, P).T)

    def tiles(w):
        w = np.asarray(w).reshape(FT, P, H // P, P)
        return np.ascontiguousarray(w.transpose(0, 3, 2, 1)).reshape(FT, P, H)

    def turned(w):
        return np.ascontiguousarray(np.asarray(w).T)

    def row(v):
        return np.ascontiguousarray(np.asarray(v).reshape(1, -1))

    arrays = {
        "x": np.ascontiguousarray(np.asarray(L0_attn_hidden_states).reshape(T, H)),
        "wq": turned(L0_attn_q_weight), "wk": turned(L0_attn_k_weight),
        "wv": turned(L0_attn_v_weight), "wo": turned(L0_attn_o_weight),
        "sq": columns(L0_attn_q_scale), "sk": columns(L0_attn_k_scale),
        "sv": row(L0_attn_v_scale), "so": row(L0_attn_o_scale),
        "gate": tiles(L0_ffn_gate_t), "up": tiles(L0_ffn_up_t), "down": turned(L0_ffn_down_t),
        "sg": columns(L0_ffn_gate_s), "su": columns(L0_ffn_up_s), "sd": row(L0_ffn_down_s),
    }
    NH = arrays["wq"].shape[1] // D
    NKV = arrays["wk"].shape[1] // D
    nc = bacc.Bacc("TRN2", target_bir_lowering=False, num_devices=1)
    args = [nc.dram_tensor(n, arrays[n].shape, mybir.dt.from_np(arrays[n].dtype), kind="ExternalInput").ap() for n in _INS]
    args.append(nc.dram_tensor("out", (T, H), F32, kind="ExternalOutput").ap())
    args.append(nc.dram_tensor("q_scratch", (NH, 3, D, T), BF16, kind="Internal").ap())
    args.append(nc.dram_tensor("k_scratch", (NKV, 6, D, T), BF16, kind="Internal").ap())
    args.append(nc.dram_tensor("o_scratch", (NH * 2 * D, T), F32, kind="Internal").ap())
    args.append(nc.dram_tensor("r_scratch", (NH, T), F32, kind="Internal").ap())
    layer_kernel(nc, *args)
    r = run_bass_kernel_spmd(nc, [arrays], core_ids=[0])
    return r.results[0]["out"].reshape(1, T, H)
```

```python
from contextlib import ExitStack

import concourse.bass as bass
from concourse import mybir

F32 = mybir.dt.float32
F16 = mybir.dt.float16
BF16 = mybir.dt.bfloat16
U8 = mybir.dt.uint8
ALU = mybir.AluOpType
ACT = mybir.ActivationFunctionType
AX = mybir.AxisListType
RMAX = bass.bass_isa.ReduceOp.max

P = 128
D = 16
EPS = 1e-5
SMALL = 1e-8
HUGE = 1e6
VTOP = 16384.0
TINY = 1e-30


def layer_kernel(nc, x, wq, wk, wv, wo, sq, sk, sv, so, gate, up, down, sg, su, sd, out,
                 q_scratch, k_scratch, o_scratch, r_scratch):
    T, H = x.shape
    HC = H // P
    TT = T // P
    HALF = T // 2
    NH, NKV = wq.shape[1] // D, wk.shape[1] // D
    KV = NKV * D
    REP = NH // NKV
    FT = gate.shape[0]
    QT = NH * D // P
    HPT = P // D
    TERMS = 6
    KROWS = TERMS * D
    SROWS = KROWS + 3
    LN = TT // 2
    UNITS = REP * HALF // P
    NQKV = (NH + 2 * NKV) * D
    SCALE = float(D) ** -0.5
    NG = NKV
    NP = NG // 2
    STEPS = 2 * TT
    FU = 2 * FT

    assert KV == P and HC * P == H and QT * P == NH * D and TT % 4 == 0

    K_, V_ = "k", "v"
    PROJ = [K_, 0, V_] + list(range(1, QT))
    order = ("F0 P0 S0 S1 E0 P1 P2 E1 G0 X0 Y0 F1 G1 F2 E2 X1 P3 F3 Y1 G2 F4 E3 V2 G3 P4 E4 P5 F5 X3 F6 Y3 "
             "F7 G4 E5 F8 X4 F9 A0 Y4 F10 G5 F11 F12 A1 A2 F13 A3 X5 F14 A4 A5 F15 A6 A7 F16 A8 A9 F17 A10 "
             "A11 F18 A12 A13 F19 A14 A15 F20 A16 A17 Y5 F21 A18 A19 F22 T0 A20 A21 F23 A22 A23 F24 A24 "
             "A25 F25 A26 A27 F26 A28 A29 F27 A30 A31 ")
    order = [(step[0], int(step[1:])) for step in order.split()]
    T_AT = [n for kind, n in order[:order.index(("T", 0))] if kind == "F"][-1]
    assert T_AT % 2 == 0
    assert order.index(("T", 0)) > order.index(("A", UNITS - 1)) and len(PROJ) == 6
    assert sum(kind == "F" for kind, _ in order) == FU and sum(kind == "A" for kind, _ in order) == 2 * UNITS
    VY = PROJ.index(V_) % 2

    NORM = [(t, 0, T) for t in range(QT - 1)] + [(QT - 1, 0, HALF), (QT - 1, HALF, HALF)]
    NU = len(NORM)
    O_INVERT, O_NORM, O_SPLIT = [15, 19, 23, 27], [17, 21, 25, 29], [18, 22, 26, 30]
    FILL = 4
    FILLS = [(i, f, part) for i in range(FILL) for f in range(FT) for part in range(2)]
    D_OUT = [20, 24, 28]
    tail = "O0 C0 O1 C1 O2 C2 O3 D4 D5 O4 O5 D6 O6 D7 O7"
    tail = [(step[0], int(step[1:])) for step in tail.split()]

    T_STEP = 1

    def at(gp, s):
        gp = gp + s // (2 * STEPS)
        s = s % (2 * STEPS)
        return gp, s // STEPS, s % STEPS // TT, s % TT

    with ExitStack() as ctx:
        def sb(name, shape, dt):
            return ctx.enter_context(nc.sbuf_tensor(name, shape, dt))

        def sem(name):
            return ctx.enter_context(nc.semaphore(name))

        ps = ctx.enter_context(nc.psum_tensor("ps", [P, 8, 512], F32))

        def bank_pair(r):
            return ps[:, 2 * r:2 * r + 2, :].rearrange("p b n -> p (b n)")

        ident = sb("ident", [P, P], F32)
        ones = sb("ones", [P, P], F32)
        eps = sb("eps", [P, 1], F32)
        warm = sb("warm", [P, 1], F32)
        stats = sb("stats", [P, 2, 6], F32)
        mv = sb("mv", [P, TT, 2], F32)
        std = sb("std", [P, TT], F32)
        rstd = sb("rstd", [P, TT], F32)
        half_var = sb("half_var", [P, TT], F32)
        newton = sb("newton", [P, TT], F32)
        room1 = sb("room1", [P, HC * (NQKV + H)], F32)
        wt = room1[:, 0:HC * NQKV].rearrange("p (c n) -> p c n", c=HC)
        wot = room1[:, HC * NQKV:].rearrange("p (c n) -> p c n", c=HC)
        room2 = sb("room2", [P, 2 * REP * HALF], F32)
        xp = room2[:, :].bitcast(F16).rearrange("p (a c n) -> p a c n", a=2, c=HC)
        xhi, xlo = xp[:, 0], xp[:, 1]
        probs = room2[:, :].rearrange("p (b r n) -> p b r n", b=2, r=REP)
        att = room2[:, 0:2 * H].rearrange("p (b n) -> p b n", b=2)
        room3 = sb("room3", [P, 6 * HALF], F32)
        xn = room3[:, 2 * H:6 * H].rearrange("p (b n) -> p b n", b=4)
        th = room3[:, 0:2 * HALF].rearrange("p (b n) -> p b n", b=2)
        gt = room3[:, 2 * HALF:4 * HALF].rearrange("p (b n) -> p b n", b=2)
        hb = room3[:, 4 * HALF:6 * HALF].rearrange("p (b n) -> p b n", b=2)
        oparts = room1[:, 0:QT * T].bitcast(F16).rearrange("p (t a n) -> p t a n", t=QT, a=2)

        sgn = sb("sgn", [P, HC, NQKV], F16)
        sgno = sb("sgno", [P, HC, H], F16)
        scqk = sb("scqk", [P, QT + 1], F32)
        cqk = sb("cqk", [P, QT + 1], F32)
        svb = sb("svb", [P, KV], F32)
        sob = sb("sob", [P, H], F32)
        dsb = sb("dsb", [P, H], F32)
        gsc = sb("gsc", [P, FT], F32)
        usc = sb("usc", [P, FT], F32)
        vg = sb("vg", [P, 4], F32)
        gain = sb("gain", [P, 4], F32)
        wf = sb("wf", [P, 2, 2, HC * P], F16)
        wd = sb("wd", [P, FT, H], F16)
        ffn = [room3[:, i * H:(i + 1) * H] for i in range(6)]
        ffn += [wf[:, :, :, :].rearrange("p a z n -> p (a z n)").bitcast(F32)[:, i * H:(i + 1) * H] for i in range(2)]
        hhi = sb("hhi", [P, FT, T], F16)
        hlo = sb("hlo", [P, FT, T], F16)
        xin = hlo[:, :, :].rearrange("p f n -> p (f n)").bitcast(F32)[:, 0:TT * H].rearrange("p (i n) -> p i n", i=TT)
        y = sb("y", [P, 2, T], F32)
        ga = sb("ga", [P, T], F32)
        gr = sb("gr", [P, T], F32)
        gb = sb("gb", [P, T], U8)
        parts = sb("parts", [P, 3, T], BF16)
        res = parts[:, :, :].rearrange("p a n -> p (a n)").bitcast(F32).rearrange("p (b n) -> p b n", b=3)
        qst = sb("qst", [P, 2, 2, REP, HALF], BF16)
        mags = qst[:, :, :, :, :].rearrange("p a b h n -> p (a b h n)").bitcast(F32)[:, 0:NQKV + H]
        kA = sb("kA", [P, 2, T], BF16)
        kB = sb("kB", [P, 2, T], BF16)
        vext = sb("vext", [P, TT, NKV, 2 * D], F32)
        vcur = sb("vcur", [P, 2, TT, 2 * D], F32)
        scrap = vcur[:, :, :, :].rearrange("p g k d -> p (g k d)")
        osb = sb("osb", [P, 2, HALF], F32)
        nmx = sb("nmx", [P, 2, UNITS], F32)
        shr = sb("shr", [UNITS, P], F32)
        shp = sb("shp", [UNITS, 2, 3, P], BF16)
        rsum = sb("rsum", [P, QT + 1, T // D], F32)

        x_loaded = [sem(f"x_loaded{i}") for i in range(TT)]
        qkv_loaded = sem("qkv_loaded")
        wo_loaded = sem("wo_loaded")
        vec_loaded = sem("vec_loaded")
        consts_ready = sem("consts_ready")
        kones_ready = sem("kones_ready")
        eps_ready = sem("eps_ready")
        pool_step = sem("pool_step")
        ln_step = sem("ln_step")
        stats_ready = sem("stats_ready")
        std_ready = sem("std_ready")
        xn_ready = sem("xn_ready")
        xT_ready = sem("xT_ready")
        xhi_ready = sem("xhi_ready")
        xlo_ready = sem("xlo_ready")
        sign_ready = sem("sign_ready")
        mag_ready = sem("mag_ready")
        sums_ready = sem("sums_ready")
        factor_step = sem("factor_step")
        factors_ready = sem("factors_ready")
        gain_ready = sem("gain_ready")
        gmax_ready = sem("gmax_ready")
        proj_ready = sem("proj_ready")
        y_ready = sem("y_ready")
        guard_step = sem("guard_step")
        guarded = sem("guarded")
        hi_ready = sem("hi_ready")
        rest_ready = sem("rest_ready")
        mid_ready = sem("mid_ready")
        split_done = sem("split_done")
        k_stored = sem("k_stored")
        q_stored = sem("q_stored")
        vext_ready = sem("vext_ready")
        vcur_ready = sem("vcur_ready")
        wf_loaded = [sem(f"wf_loaded{i}") for i in range(2)]
        wd_loaded = sem("wd_loaded")
        gate_ready = sem("gate_ready")
        up_ready = sem("up_ready")
        th_ready = sem("th_ready")
        gt_ready = sem("gt_ready")
        h_ready = sem("h_ready")
        hhi_ready = sem("hhi_ready")
        hlo_ready = sem("hlo_ready")
        q_loaded = [[sem(f"q_loaded{a}{b}") for b in range(2)] for a in range(2)]
        kA_loaded = [sem(f"kA_loaded{a}") for a in range(2)]
        kB_loaded = [sem(f"kB_loaded{a}") for a in range(2)]
        shift_loaded = [[sem(f"shift_loaded{a}{b}") for b in range(2)] for a in range(2)]
        rows_ready = sem("rows_ready")
        rows_free = sem("rows_free")
        maxT_ready = sem("maxT_ready")
        maxT_free = sem("maxT_free")
        shift_step = sem("shift_step")
        shift_ready = sem("shift_ready")
        scores_ready = sem("scores_ready")
        scores_free = sem("scores_free")
        probs_free = sem("probs_free")
        pv_free = sem("pv_free")
        osb_free = [sem(f"osb_free{i}") for i in range(2)]
        sums_loaded = [sem(f"sums_loaded{u}") for u in range(NU)]
        rsum_ready = sem("rsum_ready")
        rsum_stored = [sem(f"rsum_stored{u}") for u in range(NU)]
        num_loaded = [sem(f"num_loaded{u}") for u in range(NU)]
        rec_loaded = [sem(f"rec_loaded{u}") for u in range(NU)]
        vmax_ready = sem("vmax_ready")
        vred_ready = sem("vred_ready")
        vscale_ready = sem("vscale_ready")
        normed = sem("normed")
        o_hi = sem("o_hi")
        o_split = sem("o_split")
        down_ready = sem("down_ready")
        oproj_ready = sem("oproj_ready")
        att_ready = sem("att_ready")
        ff_ready = sem("ff_ready")
        res_loaded = [sem(f"res_loaded{i}") for i in range(3)]
        res_added = sem("res_added")
        out_ready = sem("out_ready")
        out_stored = sem("out_stored")

        def normalize_io(eng, u):
            t, c0, n = NORM[u]
            for hf in range((c0 + n) // HALF):
                eng.wait_ge(osb_free[hf], 16 * (2 * t + 3))
            heads = o_scratch.rearrange("(h z d) n -> h z d n", z=2, d=D)[t * HPT:(t + 1) * HPT]
            eng.dma_start(rsum[:, u, 0:n // D],
                          heads[:, 1, 0, c0:c0 + n].rearrange("h (b n) -> h b n", b=D)).then_inc(sums_loaded[u], 16)
            if t >= 2:
                eng.wait_ge(o_split, t - 1)
            eng.dma_start(y[:, t % 2, c0:c0 + n], heads[:, 0, :, c0:c0 + n]).then_inc(num_loaded[u], 16)
            eng.wait_ge(rsum_ready, u + 1)
            rec = r_scratch[t * HPT:(t + 1) * HPT, c0:c0 + n]
            eng.dma_start(rec.rearrange("h (b n) -> h b n", b=D), rsum[:, u, 0:n // D]).then_inc(rsum_stored[u], 16)
            eng.wait_ge(rsum_stored[u], 16)
            if t >= 1:
                eng.wait_ge(normed, t)
            eng.dma_start(ga[:, c0:c0 + n], rec.unsqueeze(1).to_broadcast([HPT, D, n])).then_inc(rec_loaded[u], 16)

        x_v = x.rearrange("(i p) h -> i p h", p=P)
        block = ctx.enter_context(nc.Block())

        @block.sync
        def _(sp):
            def load_queries(g, par, hf):
                src = q_scratch[bass.ds(g * REP, REP), :, :, hf * HALF:(hf + 1) * HALF]
                row = 0
                for n in (3, 2, 1):
                    sp.dma_start(qst[row:row + n * D, par, hf],
                                 src[:, 3 - n:3].rearrange("h t d n -> (t d) h n")).then_inc(q_loaded[par][hf], 16)
                    row += n * D

            def load_keys(buf, loaded, g, par):
                sp.dma_start(buf[0:KROWS, par, :],
                             k_scratch[bass.ds(g, 1)].rearrange("g t d n -> (g t d) n")).then_inc(loaded[par], 16)

            def load_shift(v, par, hf):
                sp.wait_ge(shift_ready, v + 1)
                for part in range(3):
                    dst = qst[KROWS + part:KROWS + part + 1, par, hf].rearrange("p h n -> p (h n)")
                    sp.dma_start(dst, shp[:, hf, part, :]).then_inc(shift_loaded[par][hf], 16)

            def load_weights(w_, c0):
                sp.dma_start(wt[:, :, c0:c0 + w_.shape[1]],
                             w_.rearrange("(c p) o -> p c o", p=P)).then_inc(qkv_loaded, 16)

            sp.sem_inc(rows_free, 2)
            sp.sem_inc(maxT_free, 1)
            sp.sem_inc(scores_free, 2)
            sp.sem_inc(probs_free, 2)
            sp.sem_inc(pv_free, 2)
            for b in range(2):
                sp.sem_inc(osb_free[b], 16)

            for i in range(TT):
                sp.dma_start(xin[:, i, :], x_v[i]).then_inc(x_loaded[i], 16)
            load_weights(wk, NH * D)
            load_weights(wq, 0)
            load_weights(wv, NH * D + KV)
            sp.dma_start(wot[:, :, :], wo.rearrange("(c p) o -> p c o", p=P)).then_inc(wo_loaded, 16)

            splits = 0
            for what in PROJ:
                if what == V_:
                    continue
                splits += 1
                sp.wait_ge(mid_ready, splits)
                sp.wait_ge(split_done, splits)
                if what == K_:
                    for term, part in enumerate([0, 1, 2, 0, 1, 0]):
                        sp.dma_start(k_scratch[:, term], parts[:, part, :]).then_inc(k_stored, 16)
                    sp.wait_ge(k_stored, 16 * TERMS)
                    for par in range(2):
                        load_keys(kA, kA_loaded, par, par)
                        load_keys(kB, kB_loaded, par, par)
                else:
                    for part in range(3):
                        sp.dma_start(q_scratch[what * HPT:(what + 1) * HPT, 2 - part], parts[:, part, :]).then_inc(q_stored, 16)
                    if what == 0:
                        sp.wait_ge(q_stored, 48)
                        for g in range(2):
                            for hf in range(2):
                                load_queries(g, g, hf)
            sp.wait_ge(q_stored, 48 * QT)
            load_shift(0, 0, 0)

            def half_ended(gp, s, last):
                _, par, hf, _ = at(gp, s - 1)
                v = gp * 4 + s // TT - 1
                g = gp * 2 + par
                if not last:
                    sp.wait_ge(scores_ready, (v + 1) * REP * TT)
                    load_queries(g + 2, par, hf)
                    if hf == 0:
                        sp.wait_ge(rows_ready, (g + 1) * 2 * UNITS)
                        load_keys(kA, kA_loaded, g + 2, par)
                    else:
                        load_keys(kB, kB_loaded, g + 2, par)
                if not last or par == 0:
                    load_shift(v + 2, 1 - par, hf)
                sp.wait_ge(pv_free, v + 3)
                sp.dma_start(o_scratch[bass.ds(g * (REP * 2 * D), REP * 2 * D), hf * HALF:(hf + 1) * HALF],
                             osb[:, hf, :]).then_inc(osb_free[hf], 16)

            load_shift(1, 0, 1)
            with sp.Fori(0, NP - 1) as gp:
                for s in range(TT, 2 * STEPS + 1, TT):
                    half_ended(gp, s, False)

            for s in range(TT, 2 * STEPS + 1, TT):
                half_ended(NP - 1, s, True)
                if s >= STEPS + TT:
                    normalize_io(sp, QT - 1 + (s - STEPS - TT) // TT)
            for kind, i in tail:
                if kind == "O":
                    sp.wait_ge(out_ready, i + 1)
                    sp.dma_start(out.rearrange("(i p) h -> i p h", p=P)[i], ffn[i]).then_inc(out_stored, 16)
            sp.wait_ge(out_stored, 16 * TT)

        @block.gpsimd
        def _(pool):
            def add_residual(i):
                pool.wait_ge(ff_ready, i + 1)
                pool.wait_ge(res_loaded[i % 3], 16 * (i // 3 + 1))
                nc.gpsimd.tensor_tensor(ffn[i], ffn[i], res[:, i % 3, :], ALU.add).then_inc(res_added, 1)

            def load_ffn(f):
                pool.dma_start(wf[:, f % 2, 0, :], gate[f]).then_inc(wf_loaded[f % 2], 16)
                pool.dma_start(wf[:, f % 2, 1, :], up[f]).then_inc(wf_loaded[f % 2], 16)

            nc.gpsimd.memset(ident[:, :], 0.0).then_inc(pool_step, 1)
            pool.wait_ge(pool_step, 1)
            nc.gpsimd.affine_select(out=ident[:, :], in_=ident[:, :], compare_op=ALU.not_equal, fill=1.0, base=0,
                                    pattern=[[-1, P]], channel_multiplier=1).then_inc(consts_ready, 1)
            nc.gpsimd.memset(ones[:, :], 1.0).then_inc(consts_ready, 1)
            load_ffn(0)
            load_ffn(1)
            nc.gpsimd.memset(vext[:, :, :, :], 1.0).then_inc(consts_ready, 1)
            pool.wait_ge(gain_ready, 1)
            nc.gpsimd.partition_all_reduce(gain[:, 1:2], gain[:, 0:1], P, RMAX).then_inc(gmax_ready, 1)

            def hidden_low(w):
                f, hf = w // 2, w % 2
                pool.wait_ge(hhi_ready, w + 1)
                nc.gpsimd.tensor_tensor(hlo[:, f, hf * HALF:(hf + 1) * HALF], hb[:, w % 2, :],
                                        hhi[:, f, hf * HALF:(hf + 1) * HALF], ALU.subtract).then_inc(hlo_ready, 1)

            for kind, w in order:
                if kind == "V":
                    pool.wait_ge(vmax_ready, 1)
                    nc.gpsimd.partition_all_reduce(vg[:, 1:2], vg[:, 0:1], P, RMAX).then_inc(vred_ready, 1)
                if kind != "F":
                    continue
                f, hf = w // 2, w % 2
                if hf == 0 and 1 <= f < FT - 1:
                    pool.wait_ge(up_ready, w)
                    load_ffn(f + 1)
                if w == 3:
                    pool.dma_start(wd[:, :, :], down.rearrange("(f p) h -> p f h", p=P)).then_inc(wd_loaded, 16)
                if w >= 1:
                    hidden_low(w - 1)
            hidden_low(FU - 1)
            pool.wait_ge(vext_ready, 1)
            for g in range(2):
                nc.gpsimd.tensor_copy(vcur[:, g, :, :], vext[:, :, g, :]).then_inc(vcur_ready, 1)
            with pool.Fori(1, NP) as gp:
                for par in range(2):
                    g = gp * 2 + par
                    pool.wait_ge(probs_free, 2 + STEPS * (g - 1))
                    nc.gpsimd.tensor_copy(vcur[:, par, :, :],
                                          vext[:, :, bass.ds(g, 1), :].rearrange("p k g d -> p k (g d)")).then_inc(vcur_ready, 1)
            for u in range(QT - 1):
                normalize_io(pool, u)
            for i in range(TT):
                if i >= 3:
                    pool.wait_ge(res_added, i - 2)
                pool.dma_start(res[:, i % 3, :], x_v[i]).then_inc(res_loaded[i % 3], 16)
                if i >= 2:
                    add_residual(i - 2)
            for i in range(TT - 2, TT):
                add_residual(i)

        @block.scalar
        def _(act):
            act.wait_ge(eps_ready, 1)
            nc.scalar.activation(warm[:, :], eps[:, :], ACT.Sqrt)
            act.dma_start(scqk[:, 0:QT], sq).then_inc(vec_loaded, 16)
            act.dma_start(scqk[:, QT:QT + 1], sk).then_inc(vec_loaded, 16)
            act.dma_start(svb[:, :], sv.to_broadcast([P, KV])).then_inc(vec_loaded, 16)
            act.dma_start(sob[:, :], so.to_broadcast([P, H])).then_inc(vec_loaded, 16)
            act.dma_start(dsb[:, :], sd.to_broadcast([P, H])).then_inc(vec_loaded, 16)
            act.dma_start(gsc[:, :], sg).then_inc(vec_loaded, 16)
            act.dma_start(usc[:, :], su).then_inc(vec_loaded, 16)
            def xhi_copy(i):
                act.wait_ge(xT_ready, i + 1)
                nc.scalar.copy(xhi[:, :, i * P:(i + 1) * P],
                               ps[:, i % 4, :].rearrange("p (c n) -> p c n", c=HC)).then_inc(xhi_ready, 1)

            for b in range(TT // LN):
                act.wait_ge(stats_ready, LN * (b + 1))
                nc.scalar.activation(std[:, LN * b:LN * (b + 1)], mv[:, LN * b:LN * (b + 1), 1], ACT.Sqrt,
                                     bias=eps[:, 0:1]).then_inc(std_ready, 1)
                for i in range(LN * b - (b > 0), LN * (b + 1) - (b == 0)):
                    xhi_copy(i)
            act.wait_ge(qkv_loaded, 48)
            for c0, c1 in ((NH * D, NQKV), (0, NH * D)):
                nc.scalar.activation(sgn[:, :, c0:c1], wt[:, :, c0:c1], ACT.Sign).then_inc(sign_ready, 1)
            act.wait_ge(wo_loaded, 16)
            nc.scalar.activation(sgno[:, :, :], wot, ACT.Sign).then_inc(sign_ready, 1)

            def hidden_high(n):
                f, hf = n // 2, n % 2
                act.wait_ge(h_ready, n + 1)
                nc.scalar.copy(hhi[:, f, hf * HALF:(hf + 1) * HALF], hb[:, n % 2, :]).then_inc(hhi_ready, 1)

            splits = 0
            for kind, n in order:
                if kind == "E" and PROJ[n] != V_:
                    col = QT if PROJ[n] == K_ else PROJ[n]
                    act.wait_ge(proj_ready, n + 1)
                    act.wait_ge(factors_ready, 2)
                    if n >= 2:
                        act.wait_ge(split_done, sum(1 for m in PROJ[:n - 1] if m != V_))
                        act.wait_ge(guarded, n - 1)
                        if PROJ[n - 2] == V_:
                            act.wait_ge(vext_ready, 1)
                    nc.scalar.activation(y[:, n % 2, :], bank_pair(n % 2), ACT.Copy,
                                         scale=cqk[:, col:col + 1]).then_inc(y_ready, 1)
                elif kind == "V":
                    act.wait_ge(vscale_ready, 1)
                    act.wait_ge(consts_ready, 3)
                    nc.scalar.activation(vext[:, :, :, 0:D].rearrange("p k g d -> p (k g) d"),
                                         y[:, VY, :].rearrange("p (m d) -> p m d", d=D), ACT.Copy,
                                         scale=vg[:, 3:4]).then_inc(vext_ready, 1)
                elif kind == "X":
                    splits += 1
                    act.wait_ge(guarded, n + 1)
                    if splits == 2:
                        act.wait_ge(k_stored, 16 * TERMS)
                    elif splits > 2:
                        act.wait_ge(q_stored, 48 * (splits - 2))
                    nc.scalar.copy(parts[:, 0, :], y[:, n % 2, :]).then_inc(hi_ready, 1)
                elif kind == "Y":
                    act.wait_ge(rest_ready, splits)
                    nc.scalar.copy(parts[:, 1, :], gr[:, :]).then_inc(mid_ready, 1)
                elif kind == "F":
                    f = n // 2
                    if n >= 1:
                        hidden_high(n - 1)
                    act.wait_ge(gate_ready, n + 1)
                    if n == 0:
                        act.wait_ge(factors_ready, 1)
                    if n >= 2:
                        act.wait_ge(gt_ready, n - 1)
                    nc.scalar.activation(th[:, n % 2, :], ps[:, 4 + 2 * (n % 2), :], ACT.Tanh,
                                         scale=gsc[:, f:f + 1]).then_inc(th_ready, 1)
            hidden_high(FU - 1)

            def exps(gp, s):
                _, _, _, kt = at(gp, s)
                step = gp * (2 * STEPS) + s
                act.wait_ge(probs_free, step + 1)
                for r in range(REP):
                    act.wait_ge(scores_ready, step * REP + r + 1)
                    nc.scalar.activation(probs[:, s % 2, r, :], ps[:, 4 + r % 2, :], ACT.Exp,
                                         scale=SCALE).then_inc(scores_free, 1)

            def take_output(gp, s):
                _, par, hf, _ = at(gp, s - 1)
                v = gp * 4 + s // TT - 1
                act.wait_ge(probs_free, (v + 1) * TT + 2)
                act.wait_ge(osb_free[hf], 16 * (gp * 2 + par + 1))
                nc.scalar.copy(osb[:, hf, :], ps[:, 6 + hf, :]).then_inc(pv_free, 1)

            def o_high(u):
                t, c0, n = NORM[u]
                act.wait_ge(normed, u + 1)
                nc.scalar.copy(oparts[:, t, 0, c0:c0 + n], y[:, t % 2, c0:c0 + n]).then_inc(o_hi, 1)

            act.wait_ge(up_ready, FU)
            exps(0, 0)
            with act.Fori(0, NP - 1) as gp:
                for s in range(1, 2 * STEPS + 1):
                    exps(gp, s)
                    if s % TT == 0:
                        take_output(gp, s)
            for s in range(1, 2 * STEPS + 1):
                if s < 2 * STEPS:
                    exps(NP - 1, s)
                if s % TT == 0:
                    take_output(NP - 1, s)
                if s in O_SPLIT:
                    o_high(O_SPLIT.index(s))
            for u in range(len(O_SPLIT), NU):
                o_high(u)

        @block.vector
        def _(dve):
            nc.vector.memset(eps[:, :], EPS).then_inc(eps_ready, 1)
            nc.vector.memset(kB[KROWS:P, :, :], 1.0).then_inc(kones_ready, 1)

            ln = 0

            def ln_result(ins):
                nonlocal ln
                ln += 1
                ins.then_inc(ln_step, 1)
                dve.wait_ge(ln_step, ln)

            def x_stats(i):
                dve.wait_ge(x_loaded[i], 16)
                ln_result(nc.vector.bn_stats(stats[:, i % 2, :], xin[:, i, :]))
                nc.vector.bn_aggr(mv[:, i, :], stats[:, i % 2, :]).then_inc(stats_ready, 1)

            def inverse_std(b):
                of = slice(LN * b, LN * (b + 1))
                ln_result(nc.vector.tensor_scalar(half_var[:, of], mv[:, of, 1], EPS, -0.5, ALU.add, ALU.mult))
                dve.wait_ge(std_ready, b + 1)
                ln_result(nc.vector.reciprocal(rstd[:, of], std[:, of]))
                ln_result(nc.vector.tensor_tensor(newton[:, of], rstd[:, of], rstd[:, of], ALU.mult))
                ln_result(nc.vector.tensor_tensor(newton[:, of], newton[:, of], half_var[:, of], ALU.mult))
                ln_result(nc.vector.scalar_tensor_tensor(out=rstd[:, of], in0=newton[:, of], scalar=1.5, in1=rstd[:, of],
                                                         op0=ALU.add, op1=ALU.mult))

            def normalize(i):
                if i >= 4:
                    dve.wait_ge(xT_ready, i - 3)
                nc.vector.tensor_scalar(xn[:, i % 4, :], xin[:, i, :], mv[:, i, 0:1], rstd[:, i:i + 1],
                                        ALU.subtract, ALU.mult).then_inc(xn_ready, 1)

            def x_low(i):
                dve.wait_ge(xhi_ready, i + 1)
                nc.vector.tensor_tensor(xlo[:, :, i * P:(i + 1) * P],
                                        ps[:, i % 4, :].rearrange("p (c n) -> p c n", c=HC),
                                        xhi[:, :, i * P:(i + 1) * P], ALU.subtract).then_inc(xlo_ready, 1)

            for i in range(LN):
                x_stats(i)
            dve.wait_ge(stats_ready, LN)
            inverse_std(0)
            for i in range(LN):
                normalize(i)
                x_stats(LN + i)
            x_low(0)
            x_low(1)
            dve.wait_ge(stats_ready, TT)
            inverse_std(1)
            for i in range(LN, TT):
                normalize(i)
                x_low(i - 2)
            x_low(TT - 2)
            x_low(TT - 1)

            steps = 0

            def step(ins):
                nonlocal steps
                steps += 1
                ins.then_inc(factor_step, 1)
                dve.wait_ge(factor_step, steps)

            def magnitudes(w_, c0):
                n = w_.shape[2]
                nc.vector.tensor_reduce(mags[:, c0:c0 + n], w_.rearrange("p c n -> p n c"), AX.X, ALU.add,
                                        apply_absolute_value=True).then_inc(mag_ready, 1)

            dve.wait_ge(vec_loaded, 16 * 7)
            step(nc.vector.tensor_tensor(usc[:, :], usc[:, :], gsc[:, :], ALU.mult))
            nc.vector.tensor_reduce(gain[:, 0:1], usc[:, :], AX.X, ALU.max, apply_absolute_value=True).then_inc(gain_ready, 1)
            step(nc.vector.tensor_scalar(gsc[:, :], gsc[:, :], 0.5, None, ALU.mult))
            dve.wait_ge(gmax_ready, 1)
            step(nc.vector.tensor_scalar(gain[:, 2:3], gain[:, 1:2], 8.0, 1e-30, ALU.mult, ALU.max))
            step(nc.vector.reciprocal(gain[:, 3:4], gain[:, 2:3]))
            step(nc.vector.tensor_scalar(usc[:, :], usc[:, :], gain[:, 3:4], 0.5, ALU.mult, ALU.mult))
            nc.vector.tensor_scalar(dsb[:, :], dsb[:, :], gain[:, 2:3], None, ALU.mult).then_inc(factors_ready, 1)

            dve.wait_ge(qkv_loaded, 48)
            magnitudes(wt, 0)
            dve.wait_ge(wo_loaded, 16)
            magnitudes(wot, NQKV)

            guards = 0

            def guard(v_, n_):
                nonlocal guards
                mask, repl, less = gb[:, 0:n_], ga[:, 0:n_], gr[:, 0:n_]
                nc.vector.tensor_scalar(repl, v_, 0.0, HUGE, ALU.is_gt, ALU.mult).then_inc(guard_step, 1)
                nc.vector.tensor_scalar(less, v_, 0.0, HUGE, ALU.is_lt, ALU.mult).then_inc(guard_step, 1)
                nc.vector.tensor_scalar(mask, v_, 0.0, 0.0, ALU.mult, ALU.not_equal).then_inc(guard_step, 1)
                dve.wait_ge(guard_step, guards + 2)
                nc.vector.tensor_tensor(repl, repl, less, ALU.subtract).then_inc(guard_step, 1)
                guards += 4
                dve.wait_ge(guard_step, guards)
                return nc.vector.copy_predicated(v_, mask, repl)

            def row_max(n, hf, idx):
                dve.wait_ge(rows_ready, n + 1)
                nc.vector.tensor_reduce(nmx[:, hf, idx:idx + 1], bank_pair(idx % 2), AX.X, ALU.max,
                                        negate=True).then_inc(rows_free, 1)

            def split_max(v, hf, stage):
                maxT = ps[0:UNITS, 6 + hf, 0:P]
                if stage == 0:
                    dve.wait_ge(maxT_ready, v + 1)
                    nc.vector.tensor_copy(shp[:, hf, 0, :], maxT).then_inc(shift_step, 1)
                elif stage == 1:
                    dve.wait_ge(shift_step, 2 * v + 1)
                    nc.vector.tensor_tensor(shr[:, :], maxT, shp[:, hf, 0, :], ALU.subtract).then_inc(maxT_free, 1)
                elif stage == 2:
                    dve.wait_ge(maxT_free, v + 2)
                    nc.vector.tensor_copy(shp[:, hf, 1, :], shr[:, :]).then_inc(shift_step, 1)
                else:
                    dve.wait_ge(shift_step, 2 * v + 2)
                    nc.vector.tensor_tensor(shp[:, hf, 2, :], shr[:, :], shp[:, hf, 1, :], ALU.subtract).then_inc(shift_ready, 1)

            splits = 0
            for kind, n in order:
                if kind == "E" and PROJ[n] == V_:
                    dve.wait_ge(proj_ready, n + 1)
                    dve.wait_ge(factors_ready, 3)
                    dve.wait_ge(mid_ready, splits)
                    nc.vector.tensor_tensor(y[:, n % 2, :].rearrange("p (k m) -> p k m", m=KV),
                                            bank_pair(n % 2).rearrange("p (k m) -> p k m", m=KV),
                                            svb[:, :].unsqueeze(1).to_broadcast([P, TT, KV]),
                                            ALU.mult).then_inc(y_ready, 1)
                elif kind == "S" and n == 0:
                    dve.wait_ge(sums_ready, 1)
                    step(nc.vector.tensor_scalar(cqk[:, :], ps[:, 7, 0:QT + 1], 1.0 / H, SMALL, ALU.mult, ALU.max))
                    nc.vector.tensor_tensor(cqk[:, :], cqk[:, :], scqk[:, :], ALU.mult).then_inc(factors_ready, 1)
                    step(nc.vector.tensor_scalar(ga[:, 0:KV], ps[:, 7, KV:2 * KV], 1.0 / H, SMALL, ALU.mult, ALU.max))
                    nc.vector.tensor_tensor(svb[:, :], ga[:, 0:KV], svb[:, :], ALU.mult).then_inc(factors_ready, 1)
                elif kind == "S":
                    dve.wait_ge(sums_ready, 2)
                    step(nc.vector.tensor_scalar(scrap, ps[:, 6, :], 1.0 / H, SMALL, ALU.mult, ALU.max))
                    nc.vector.tensor_tensor(sob[:, :], scrap, sob[:, :], ALU.mult).then_inc(factors_ready, 1)
                elif kind == "G":
                    dve.wait_ge(y_ready, n + 1)
                    if n == 0:
                        dve.wait_ge(factors_ready, 3)
                    else:
                        dve.wait_ge(guarded, n)
                        dve.wait_ge(split_done, splits)
                    guard(y[:, n % 2, :], T).then_inc(guarded, 1)
                    if PROJ[n] == V_:
                        dve.wait_ge(guarded, n + 1)
                        nc.vector.tensor_reduce(vg[:, 0:1], y[:, n % 2, :], AX.X, ALU.max,
                                                apply_absolute_value=True).then_inc(vmax_ready, 1)
                elif kind == "X":
                    splits += 1
                    dve.wait_ge(hi_ready, splits)
                    nc.vector.tensor_tensor(gr[:, :], y[:, n % 2, :], parts[:, 0, :], ALU.subtract).then_inc(rest_ready, 1)
                elif kind == "Y":
                    dve.wait_ge(mid_ready, splits)
                    nc.vector.tensor_tensor(parts[:, 2, :], gr[:, :], parts[:, 1, :], ALU.subtract).then_inc(split_done, 1)
                elif kind == "F":
                    f, hf = n // 2, n % 2
                    dve.wait_ge(th_ready, n + 1)
                    nc.vector.scalar_tensor_tensor(out=gt[:, n % 2, :], in0=th[:, n % 2, :], scalar=1.0,
                                                   in1=ps[:, 4 + 2 * (n % 2), :], op0=ALU.add,
                                                   op1=ALU.mult).then_inc(gt_ready, 1)
                    dve.wait_ge(gt_ready, n + 1)
                    dve.wait_ge(up_ready, n + 1)
                    if n >= 2:
                        dve.wait_ge(hlo_ready, n - 1)
                    nc.vector.scalar_tensor_tensor(out=hb[:, n % 2, :], in0=ps[:, 5 + 2 * (n % 2), :],
                                                   scalar=usc[:, f:f + 1], in1=gt[:, n % 2, :],
                                                   op0=ALU.mult, op1=ALU.mult).then_inc(h_ready, 1)
                elif kind == "V":
                    dve.wait_ge(vred_ready, 1)
                    step(nc.vector.tensor_scalar(vg[:, 2:3], vg[:, 1:2], TINY, 1.0 / VTOP, ALU.max, ALU.mult))
                    nc.vector.reciprocal(vg[:, 3:4], vg[:, 2:3]).then_inc(vscale_ready, 1)
                    nc.vector.tensor_scalar(sob[:, :], sob[:, :], vg[:, 2:3], None, ALU.mult).then_inc(vscale_ready, 1)
                elif kind == "A":
                    row_max(n, n // UNITS, n % UNITS)
                elif kind == "T":
                    for stage in range(4):
                        split_max(0, 0, stage)

            def step_rows(gp, s, last):
                gp_, par, hf, kt = at(gp, s)
                if not (last and (par == 1 or s == 2 * STEPS)):
                    ga_ = gp_ * 2 + par + 1
                    for j in range(2):
                        idx = 2 * kt + j
                        row_max(ga_ * (2 * UNITS) + hf * UNITS + idx, hf, idx)
                if T_STEP < kt <= T_STEP + 4 and not (last and s >= STEPS + TT):
                    split_max(gp * 4 + s // TT + 1, 1 - hf, kt - T_STEP - 1)

            def invert(u):
                dve.wait_ge(sums_loaded[u], 16)
                n = NORM[u][2] // D
                nc.vector.reciprocal(rsum[:, u, 0:n], rsum[:, u, 0:n]).then_inc(rsum_ready, 1)

            def normalize_output(u):
                t, c0, n = NORM[u]
                dve.wait_ge(num_loaded[u], 16)
                dve.wait_ge(rec_loaded[u], 16)
                nc.vector.tensor_tensor(y[:, t % 2, c0:c0 + n], y[:, t % 2, c0:c0 + n], ga[:, c0:c0 + n],
                                        ALU.mult).then_inc(normed, 1)

            def o_low(u):
                t, c0, n = NORM[u]
                dve.wait_ge(o_hi, u + 1)
                nc.vector.tensor_tensor(oparts[:, t, 1, c0:c0 + n], y[:, t % 2, c0:c0 + n], oparts[:, t, 0, c0:c0 + n],
                                        ALU.subtract).then_inc(o_split, 1)

            def down_out(i):
                dve.wait_ge(down_ready, i + 1)
                nc.vector.tensor_tensor(ffn[i], ps[:, i, :], dsb[:, :], ALU.mult).then_inc(ff_ready, 1)

            def rows_out(i):
                dve.wait_ge(oproj_ready, i + 1)
                if i >= 2:
                    dve.wait_ge(out_ready, i - 1)
                nc.vector.tensor_tensor(att[:, i % 2, :], ps[:, i % FILL, :], sob[:, :], ALU.mult).then_inc(att_ready, 1)
                dve.wait_ge(att_ready, 2 * i + 1)
                guard(att[:, i % 2, :], H).then_inc(att_ready, 1)
                dve.wait_ge(att_ready, 2 * i + 2)
                dve.wait_ge(res_added, i + 1)
                nc.vector.tensor_tensor(ffn[i], ffn[i], att[:, i % 2, :], ALU.add).then_inc(out_ready, 1)

            step_rows(0, 0, False)
            with dve.Fori(0, NP - 1) as gp:
                for s in range(1, 2 * STEPS + 1):
                    step_rows(gp, s, False)
            for s in range(1, 2 * STEPS):
                step_rows(NP - 1, s, True)
                if s in O_INVERT:
                    invert(O_INVERT.index(s))
                if s in O_NORM:
                    normalize_output(O_NORM.index(s))
                if s in O_SPLIT:
                    o_low(O_SPLIT.index(s))
                if s in D_OUT:
                    down_out(D_OUT.index(s))

            down_out(FILL - 1)
            for kind, i in tail:
                if kind == "C":
                    (invert, normalize_output, o_low)[i](NU - 1)
                elif kind == "D":
                    down_out(i)
                else:
                    rows_out(i)

        @block.tensor
        def _(pe):
            pe.wait_ge(consts_ready, 1)
            for i in range(TT):
                pe.wait_ge(xn_ready, i + 1)
                if i >= 4:
                    pe.wait_ge(xlo_ready, i - 3)
                for c in range(HC):
                    mm = nc.tensor.transpose(ps[:, i % 4, c * P:(c + 1) * P], xn[:, i % 4, c * P:(c + 1) * P], ident[:, :])
                mm.then_inc(xT_ready, 1)

            def sum_magnitudes(part):
                pe.wait_ge(mag_ready, part + 1)
                if part == 0:
                    pe.wait_ge(consts_ready, 2)
                    for col in range(QT + 1):
                        nc.tensor.matmul(ps[:, 7, col:col + 1], mags[:, col * P:(col + 1) * P], ones[:, 0:1],
                                         start=True, stop=True)
                    mm = nc.tensor.matmul(ps[:, 7, KV:2 * KV], ones[:, :], mags[:, NH * D + KV:NQKV], start=True, stop=True)
                else:
                    mm = nc.tensor.matmul(ps[:, 6, :], ones[:, :], mags[:, NQKV:], start=True, stop=True)
                mm.then_inc(sums_ready, 1)

            def project(n):
                what = PROJ[n]
                pe.wait_ge(sign_ready, 1 if n == 0 else 2)
                pe.wait_ge(xlo_ready, TT)
                if n >= 2:
                    pe.wait_ge(y_ready, n - 1)
                if what == V_:
                    for k in range(TT):
                        for c in range(HC):
                            for xs in (xhi, xlo):
                                mm = nc.tensor.matmul(bank_pair(n % 2)[:, k * KV:(k + 1) * KV], xs[:, c, k * P:(k + 1) * P],
                                                      sgn[:, c, NH * D + KV:NQKV], start=(c == 0 and xs is xhi),
                                                      stop=(c == HC - 1 and xs is xlo))
                else:
                    c0 = NH * D if what == K_ else what * P
                    for hf in range(2):
                        for c in range(HC):
                            for xs in (xhi, xlo):
                                mm = nc.tensor.matmul(ps[:, 2 * (n % 2) + hf, :], sgn[:, c, c0:c0 + P],
                                                      xs[:, c, hf * HALF:(hf + 1) * HALF],
                                                      start=(c == 0 and xs is xhi), stop=(c == HC - 1 and xs is xlo))
                mm.then_inc(proj_ready, 1)

            def feed_forward(w):
                f, hf = w // 2, w % 2
                pe.wait_ge(wf_loaded[f % 2], 32 * (f // 2 + 1))
                pe.wait_ge(xlo_ready, LN if w == 0 else TT)
                if w == 1:
                    pe.wait_ge(factors_ready, 4)
                elif w >= 2:
                    pe.wait_ge(h_ready, w - 1)
                if w == T_AT + 1:
                    pe.wait_ge(maxT_free, 2)
                for z, ready in ((0, gate_ready), (1, up_ready)):
                    for c in range(HC):
                        for xs in (xhi, xlo):
                            mm = nc.tensor.matmul(ps[:, 4 + 2 * (w % 2) + z, :], wf[:, f % 2, z, c * P:(c + 1) * P],
                                                  xs[:, c, hf * HALF:(hf + 1) * HALF],
                                                  start=(c == 0 and xs is xhi), stop=(c == HC - 1 and xs is xlo))
                    mm.then_inc(ready, 1)

            def rows(n, par, hf, idx):
                head, qt = idx // (HALF // P), idx % (HALF // P)
                pe.wait_ge(rows_free, n + 1)
                for b in range(2):
                    mm = nc.tensor.matmul(ps[:, 2 * (idx % 2) + b, :], qst[0:KROWS, par, hf, head, qt * P:(qt + 1) * P],
                                          kA[0:KROWS, par, b * HALF:(b + 1) * HALF], start=True, stop=True)
                mm.then_inc(rows_ready, 1)

            def transpose_max(v, hf):
                pe.wait_ge(rows_free, 2 + (v + 1) * UNITS)
                pe.wait_ge(maxT_free, v + 1)
                nc.tensor.transpose(ps[0:UNITS, 6 + hf, 0:P], nmx[:, hf, :], ident[:, :]).then_inc(maxT_ready, 1)

            for kind, n in order:
                if kind == "P":
                    project(n)
                elif kind == "S":
                    sum_magnitudes(n)
                elif kind == "F":
                    feed_forward(n)
                elif kind == "A":
                    if n == 0:
                        pe.wait_ge(y_ready, len(PROJ))
                        pe.wait_ge(kA_loaded[0], 16)
                    if n % UNITS == 0:
                        pe.wait_ge(q_loaded[0][n // UNITS], 48)
                    rows(n, 0, n // UNITS, n % UNITS)
                elif kind == "T":
                    pe.wait_ge(h_ready, T_AT)
                    transpose_max(0, 0)

            def down_proj(i, f, part):
                if f == 0 and part == 0:
                    if i < 4:
                        pe.wait_ge(wd_loaded, 16)
                        pe.wait_ge(rows_free, 2 + NG * 2 * UNITS)
                    elif i < 6:
                        pe.wait_ge(scores_free, 2 + NG * STEPS * REP)
                    else:
                        pe.wait_ge(pv_free, 2 * NG + i - 5)
                mm = nc.tensor.matmul(ps[:, i, :], (hhi, hlo)[part][:, f, i * P:(i + 1) * P], wd[:, f, :],
                                      start=(f == 0 and part == 0), stop=(f == FT - 1 and part == 1))
                if f == FT - 1 and part == 1:
                    mm.then_inc(down_ready, 1)

            def scores(gp, s, last):
                gp_, par, hf, kt = at(gp, s)
                step_ = gp * (2 * STEPS) + s
                if kt == 0:
                    pe.wait_ge(q_loaded[par][hf], 48 * (gp_ + 1))
                    pe.wait_ge(shift_loaded[par][hf], 48 * (gp_ + 1))
                    if hf == 0:
                        pe.wait_ge(kB_loaded[par], 16 * (gp_ + 1))
                with_rows = not (last and par == 1)
                if with_rows and kt == 0:
                    pe.wait_ge(q_loaded[1 - par][hf], 48 * (gp_ + par + 1))
                    if hf == 0:
                        pe.wait_ge(kA_loaded[1 - par], 16 * (gp_ + par + 1))
                if not with_rows:
                    fill = list(range(len(FILLS) * (s - STEPS) // STEPS, len(FILLS) * (s - STEPS + 1) // STEPS))
                for r in range(REP):
                    pe.wait_ge(scores_free, step_ * REP + r + 1)
                    nc.tensor.matmul(ps[:, 4 + r % 2, :], kB[0:SROWS, par, kt * P:(kt + 1) * P],
                                     qst[0:SROWS, par, hf, r, :], start=True, stop=True).then_inc(scores_ready, 1)
                    if r == 0 and with_rows:
                        for idx in (2 * kt, 2 * kt + 1):
                            rows((gp_ * 2 + par + 1) * (2 * UNITS) + hf * UNITS + idx, 1 - par, hf, idx)
                    elif r == 0:
                        for n in fill:
                            down_proj(*FILLS[n])
                    elif r == 2 and s > 0:
                        times_values(gp, s - 1)
                if kt == T_STEP and not (last and s >= STEPS + TT):
                    pe.wait_ge(pv_free, gp * 4 + s // TT + 2)
                    transpose_max(gp * 4 + s // TT + 1, 1 - hf)

            def times_values(gp, s):
                gp_, par, hf, kt = at(gp, s)
                step_ = gp * (2 * STEPS) + s
                if kt == 0:
                    pe.wait_ge(pv_free, gp * 4 + s // TT + 1)
                    pe.wait_ge(maxT_free, gp * 4 + s // TT + 2)
                    if hf == 0:
                        pe.wait_ge(vcur_ready, gp * 2 + par + 1)
                pe.wait_ge(scores_free, 2 + (step_ + 1) * REP)
                for r in range(REP):
                    mm = nc.tensor.matmul(ps[32 * r:32 * r + 32, 6 + hf, :], vcur[:, par, kt, :], probs[:, s % 2, r, :],
                                          start=(kt == 0), stop=(kt == TT - 1))
                mm.then_inc(probs_free, 1)

            pe.wait_ge(h_ready, FU - 1)
            pe.wait_ge(kones_ready, 1)
            scores(0, 0, False)
            pe.wait_ge(h_ready, FU)
            with pe.Fori(0, NP - 1) as gp:
                for s in range(2 * STEPS):
                    scores(gp, s + 1, False)
            for s in range(2 * STEPS - 1):
                scores(NP - 1, s + 1, True)
            times_values(NP - 1, 2 * STEPS - 1)


            def out_proj(i):
                pe.wait_ge(sign_ready, 3)
                pe.wait_ge(o_split, NU if i >= TT // 2 else NU - 1)
                if i < FILL:
                    pe.wait_ge(ff_ready, i + 1)
                else:
                    pe.wait_ge(att_ready, 2 * (i - FILL) + 1)
                for t in range(QT):
                    for part in range(2):
                        mm = nc.tensor.matmul(ps[:, i % FILL, :], oparts[:, t, part, i * P:(i + 1) * P], sgno[:, t, :],
                                              start=(t == 0 and part == 0), stop=(t == QT - 1 and part == 1))
                mm.then_inc(oproj_ready, 1)

            for kind, i in tail:
                if kind == "O":
                    out_proj(i)
                elif kind == "D":
                    for f in range(FT):
                        for part in range(2):
                            down_proj(i, f, part)


_INS = ["x", "wq", "wk", "wv", "wo", "sq", "sk", "sv", "so", "gate", "up", "down", "sg", "su", "sd"]


def kernel(L0_attn_hidden_states, L0_attn_q_weight, L0_attn_q_scale, L0_attn_k_weight, L0_attn_k_scale,
           L0_attn_v_weight, L0_attn_v_scale, L0_attn_o_weight, L0_attn_o_scale, L0_ffn_gate_t, L0_ffn_up_t,
           L0_ffn_down_t, L0_ffn_gate_s, L0_ffn_up_s, L0_ffn_down_s):
    import numpy as np
    import concourse.bacc as bacc
    from concourse.bass_utils import run_bass_kernel_spmd

    _, T, H = L0_attn_hidden_states.shape
    FT = L0_ffn_gate_t.shape[0] // P

    def columns(v):
        return np.ascontiguousarray(np.asarray(v).reshape(-1, P).T)

    def tiles(w):
        w = np.asarray(w).reshape(FT, P, H // P, P)
        return np.ascontiguousarray(w.transpose(0, 3, 2, 1)).reshape(FT, P, H)

    def turned(w):
        return np.ascontiguousarray(np.asarray(w).T)

    def row(v):
        return np.ascontiguousarray(np.asarray(v).reshape(1, -1))

    arrays = {
        "x": np.ascontiguousarray(np.asarray(L0_attn_hidden_states).reshape(T, H)),
        "wq": turned(L0_attn_q_weight), "wk": turned(L0_attn_k_weight),
        "wv": turned(L0_attn_v_weight), "wo": turned(L0_attn_o_weight),
        "sq": columns(L0_attn_q_scale), "sk": columns(L0_attn_k_scale),
        "sv": row(L0_attn_v_scale), "so": row(L0_attn_o_scale),
        "gate": tiles(L0_ffn_gate_t), "up": tiles(L0_ffn_up_t), "down": turned(L0_ffn_down_t),
        "sg": columns(L0_ffn_gate_s), "su": columns(L0_ffn_up_s), "sd": row(L0_ffn_down_s),
    }
    NH = arrays["wq"].shape[1] // D
    NKV = arrays["wk"].shape[1] // D
    nc = bacc.Bacc("TRN2", target_bir_lowering=False, num_devices=1)
    args = [nc.dram_tensor(n, arrays[n].shape, mybir.dt.from_np(arrays[n].dtype), kind="ExternalInput").ap() for n in _INS]
    args.append(nc.dram_tensor("out", (T, H), F32, kind="ExternalOutput").ap())
    args.append(nc.dram_tensor("q_scratch", (NH, 3, D, T), BF16, kind="Internal").ap())
    args.append(nc.dram_tensor("k_scratch", (NKV, 6, D, T), BF16, kind="Internal").ap())
    args.append(nc.dram_tensor("o_scratch", (NH * 2 * D, T), F32, kind="Internal").ap())
    args.append(nc.dram_tensor("r_scratch", (NH, T), F32, kind="Internal").ap())
    layer_kernel(nc, *args)
    r = run_bass_kernel_spmd(nc, [arrays], core_ids=[0])
    return r.results[0]["out"].reshape(1, T, H)
```
